# Optimizing a Trainium2 kernel written in Bass

```python
import numpy as np
import jax
import jax.numpy as jnp

def _softmax(x, axis=-1):
    return jax.nn.softmax(x, axis=axis)

def _gelu(x):
    return jax.nn.gelu(x, approximate=True)

def _silu(x):
    return jax.nn.silu(x)

def _sigmoid(x):
    return jax.nn.sigmoid(x)

def _layernorm(x, axis=-1, eps=1e-05):
    m = jnp.mean(x, axis=axis, keepdims=True)
    v = jnp.var(x, axis=axis, keepdims=True)
    return (x - m) / jnp.sqrt(v + eps)

def _scatter_add(tgt, idx, src, axis=0):
    return tgt.at[idx].add(src)

def _segment_sum(src, seg, n):
    return jax.ops.segment_sum(src, seg, n)
kernel_name = 'mk_adj_resnorm_d2_adj_r2_68d674'

def setup_inputs(seed: int=0):
    np.random.seed(seed)
    _w = jnp.asarray

    def _rec_inputs():
        import jax
        import jax.numpy as jnp
        _gk = jax.random.key(seed)
        x = -0.000929 + 1 * jax.random.normal(jax.random.fold_in(_gk, 1), (8192, 64), jnp.float32)
        _a = jax.random.bernoulli(jax.random.fold_in(_gk, 2), 0.000488281, (8192, 8192))
        _a = jnp.logical_or(_a, jnp.swapaxes(_a, -1, -2))
        _a = jnp.logical_or(_a, jnp.eye(8192, dtype=bool))
        _af = _a.astype(jnp.float32)
        adj = _af
        return (x, adj)
    x, adj = _rec_inputs()

    def _L0_gnn_setup():
        import jax, jax.numpy as jnp
        import numpy as np
        N = 8192
        D_IN = 64
        D_OUT = 64
        EDGE_P = 0.002
        key = jax.random.key(seed)
        kx, ka, kw = jax.random.split(key, 3)
        X = jax.random.normal(kx, (N, D_IN), dtype=jnp.float32)
        adj = (jax.random.uniform(ka, (N, N)) < EDGE_P).astype(jnp.float32)
        W = jax.random.normal(kw, (D_OUT, 2 * D_IN), dtype=jnp.float32) * (1.0 / np.sqrt(2 * D_IN))
        return {'X': X, 'adj': adj, 'W': W}
    _L0_gnn_all = _L0_gnn_setup()
    _L0_gnn_in = {k: v for k, v in _L0_gnn_all.items() if k in ('W',)}
    del _L0_gnn_all

    def _L1_gnn_setup():
        import jax, jax.numpy as jnp
        import numpy as np
        N = 8192
        IN_C = 64
        OUT_C = 64
        key = jax.random.key(seed)
        k1, k2, k3 = jax.random.split(key, 3)
        x = jax.random.normal(k1, (N, IN_C), dtype=jnp.float32)
        adj = jax.random.uniform(k2, (N, N), dtype=jnp.float32)
        scale = jnp.sqrt(6.0 / (IN_C + OUT_C))
        weight = jax.random.uniform(k3, (IN_C, OUT_C), dtype=jnp.float32, minval=-scale, maxval=scale)
        return {'x': x, 'adj': adj, 'weight': weight}
    _L1_gnn_all = _L1_gnn_setup()
    _L1_gnn_in = {k: v for k, v in _L1_gnn_all.items() if k in ('weight',)}
    del _L1_gnn_all
    return {'x': x, 'adj': adj, 'L0_gnn_W': _L0_gnn_in['W'], 'L1_gnn_weight': _L1_gnn_in['weight']}

def reference(x, adj, L0_gnn_W, L1_gnn_weight):
    import jax
    import jax.numpy as jnp

    def _L0_gnn_ref(X, adj, W):
        import jax, jax.numpy as jnp
        import numpy as np
        N = 8192
        D_IN = 64
        D_OUT = 64
        EDGE_P = 0.002
        deg = jnp.sum(adj, axis=1, keepdims=True)
        nb_agg = adj @ X / jnp.maximum(deg, 1.0)
        X_cat = jnp.concatenate([X, nb_agg], axis=1)
        out = X_cat @ W.T
        return jax.nn.relu(out)

    def _L1_gnn_ref(x, adj, weight):
        import jax, jax.numpy as jnp
        import numpy as np
        N = 8192
        IN_C = 64
        OUT_C = 64
        agg = adj @ x
        return agg @ weight
    x = _layernorm(x + _L0_gnn_ref(x, adj, L0_gnn_W), axis=-1)
    x = _layernorm(x + _L1_gnn_ref(x, adj, L1_gnn_weight), axis=-1)
    return x

_drawn_inputs = setup_inputs


def setup_inputs(seed=0):
    import zlib

    import numpy as np

    out = dict(_drawn_inputs(seed))
    spreads = {}
    factors = {}
    for name, (base, spread) in spreads.items():
        noise = np.random.default_rng([zlib.crc32(name.encode()), seed]).standard_normal(out[name].shape)
        drawn = base * np.exp(spread * noise) if base else spread * noise
        out[name] = jnp.asarray(drawn.astype(out[name].dtype))
    for name, factor in factors.items():
        out[name] = (out[name] * factor).astype(out[name].dtype)
    return out
```

```python
from contextlib import ExitStack

import numpy as np
import concourse.bass as bass
from concourse import mybir

P = 128
N = 8192
D = 64
NB = N // P
NPAIR = NB // 2
EPS = 1e-5

HALF = N // 2
HB = NB // 2
SLOTS = 4

BITS = 16
WPB = P // BITS
UPB = WPB // 2
SHIFTS = 8
TWO_FP8 = 6
TWO_MASK = 0x40404040

GROUPS = 4
PPG = NPAIR // GROUPS
SPG = NB // GROUPS
LAG = 4
KNOWN = [max(0, SPG * g - LAG) for g in range(GROUPS)]

XW = 3 * D + 1
ZW = 3 * D
XZ = XW + ZW + 1

GCH = 512
GQ = GCH // P
GN = N // GCH


def pack_weights():
    w = np.zeros((P, WPB), np.float32)
    for i in range(P):
        w[i, (i % BITS) // 2] = 2.0 ** (8 * (i % 2) + i // BITS)
    return w


def gnn_kernel(nc, x, adj, w0, w1, packw_in, ident_in, out):
    fp32, bf16, u8 = mybir.dt.float32, mybir.dt.bfloat16, mybir.dt.uint8
    u16, u32, i32, fp8 = mybir.dt.uint16, mybir.dt.uint32, mybir.dt.int32, mybir.dt.float8e4
    ALU = mybir.AluOpType
    ACT = mybir.ActivationFunctionType
    AX = mybir.AxisListType.X
    ds = bass.ds

    ctx = ExitStack()
    with ctx:
        def sb(name, shape, dt):
            return ctx.enter_context(nc.sbuf_tensor(name, shape, dt))

        def pb(name, shape, dt):
            return ctx.enter_context(nc.psum_tensor(name, shape, dt))

        def sem(name):
            return ctx.enter_context(nc.semaphore(name))

        raw = [sb(f"raw{c}", [P, HALF], fp32) for c in range(SLOTS)]
        words = [sb(f"words{g}", [P, SPG, (NB - KNOWN[g]) * WPB], u16) for g in range(GROUPS)]
        words_now = sb("words_now", [P, 2, NB * WPB], u16)
        spread = sb("spread", [P, 2, NB, SHIFTS, UPB], u32)
        xz = sb("xz", [P, NB, XZ], bf16)
        resid = sb("resid", [P, NB, D], fp32)
        verdict = sb("verdict", [P, HALF], u8)
        bad = sb("bad", [P, 2 * NB], fp32)
        bad_row = sb("bad_row", [P, 1], fp32)
        flag = sb("flag", [1, 1], i32)
        ident = sb("ident", [P, P], fp32)
        packw_f = sb("packw_f", [P, WPB], fp32)
        packw = sb("packw", [P, WPB], bf16)
        ones = sb("ones", [P, 1], fp32)
        eps1 = sb("eps1", [P, 1], fp32)
        eps4 = sb("eps4", [P, 1], fp32)
        w0_sb = sb("w0_sb", [D, 2 * D], fp32)
        w0T = sb("w0T", [2 * D, D], fp32)
        w1_sb = sb("w1_sb", [D, D], fp32)
        agg = sb("agg", [P, 2, D], fp32)
        part = sb("part", [P, 2, D], fp32)
        part_kept = sb("part_kept", [P, 2, D], fp32)
        deg = sb("deg", [P, 2], fp32)
        deg_inv = sb("deg_inv", [P, 2], fp32)
        cat = sb("cat", [P, 2, 2 * D], fp32)
        catT = sb("catT", [2 * D, 2 * P], fp32)
        h = sb("h", [P, 2, D], fp32)
        stats = sb("stats", [P, 2, 6], fp32)
        meanvar = sb("meanvar", [P, 2, 2], fp32)
        std = sb("std", [P, 2], fp32)
        rstd = sb("rstd", [P, 2], fp32)
        x1 = sb("x1", [P, 2, D], fp32)
        x1_twice = sb("x1_twice", [P, 2, D], fp32)
        x1T = sb("x1T", [D, 2 * P], fp32)
        z_rest = sb("z_rest", [P, 2, D], fp32)

        ps_words = [pb(f"ps_words{i}", [P, 512], fp32) for i in range(2)]
        ps_agg = [pb(f"ps_agg{i}", [P, 512], fp32) for i in range(2)]
        ps_catT = pb("ps_catT", [P, 512], fp32)
        ps_lin0 = pb("ps_lin0", [P, 512], fp32)
        ps_x1T = pb("ps_x1T", [P, 512], fp32)
        ps_z = pb("ps_z", [P, 512], fp32)
        ps_lin0_v = ps_lin0[:, 0:2 * D].rearrange("p (a f) -> p a f", a=2)
        ps_z_v = ps_z[:, 0:2 * D].rearrange("p (a f) -> p a f", a=2)

        QX = NB // 2
        x_rest = [words[1 + q][:, :, :].rearrange("p a b -> p (a b)")[:, 0:QX * D * 2].bitcast(fp32)
                  .rearrange("p (j f) -> p j f", f=D) for q in range(2)]

        raw_in = [sem(f"raw_in{c}") for c in range(SLOTS)]
        x_in = sem("x_in")
        const_in = sem("const_in")
        out_written = sem("out_written")
        consts_made = sem("consts_made")
        w0_transposed = sem("w0_transposed")
        w0T_copied = sem("w0T_copied")
        x_hi_stored = sem("x_hi_stored")
        x_rest_made = sem("x_rest_made")
        x_mid_stored = sem("x_mid_stored")
        x_split = sem("x_split")
        half_packed = sem("half_packed")
        half_checked = sem("half_checked")
        words_copied = sem("words_copied")
        spread_done = sem("spread_done")
        product_done = sem("product_done")
        agg_read = sem("agg_read")
        deg_inverted = sem("deg_inverted")
        cat_written = sem("cat_written")
        cat_transposed = sem("cat_transposed")
        catT_copied = sem("catT_copied")
        lin0_done = sem("lin0_done")
        h_written = sem("h_written")
        stats_written = sem("stats_written")
        var_ready = sem("var_ready")
        std_ready = sem("std_ready")
        rstd_ready = sem("rstd_ready")
        normed = sem("normed")
        x1_doubled = sem("x1_doubled")
        resid_written = sem("resid_written")
        x1_transposed = sem("x1_transposed")
        x1T_copied = sem("x1T_copied")
        z_done = sem("z_done")
        z_hi_stored = sem("z_hi_stored")
        z_rest_made = sem("z_rest_made")
        z_mid_stored = sem("z_mid_stored")
        z_stored = sem("z_stored")
        bad_counted = sem("bad_counted")
        bad_summed = sem("bad_summed")
        flag_ready = sem("flag_ready")
        g_x_in = sem("g_x_in")
        g_chunk_in = sem("g_chunk_in")
        g_chunk_free = sem("g_chunk_free")
        g_row_summed = sem("g_row_summed")
        g_transposed = sem("g_transposed")
        g_copied = sem("g_copied")
        g_partial = sem("g_partial")
        g_added = sem("g_added")
        g_dve = sem("g_dve")
        g_rows_ready = sem("g_rows_ready")
        g_pe = sem("g_pe")
        g_act = sem("g_act")
        g_out = sem("g_out")

        block = ctx.enter_context(nc.Block())

        x_rows = x.rearrange("(j p) f -> p j f", p=P)
        out_rows = out.rearrange("(j p) f -> p j f", p=P)
        adj_stripes = adj.rearrange("(i p) n -> p i n", p=P)

        def apart(eng):
            eng.nop(nofuse=True)

        g_x = raw[0][:, 0:NB * D].rearrange("p (j f) -> p j f", f=D)
        g_x1 = raw[1][:, 0:NB * D].rearrange("p (j f) -> p j f", f=D)
        g_z = raw[2][:, 0:NB * D].rearrange("p (j f) -> p j f", f=D)
        g_chunk = raw[3][:, 0:GCH]
        g_chunkT = raw[3][:, GCH:2 * GCH]
        g_acc = agg[:, 0, :]
        g_rowsum = deg_inv[:, 1:2]

        @block.sync
        def _(sp):
            def load_half(t, c):
                stripe, half = 2 * t + c // 2, c % 2
                sp.dma_start(raw[c][:, :], adj_stripes[:, ds(stripe, 1), half * HALF:(half + 1) * HALF]
                             .rearrange("p a n -> p (a n)")).then_inc(raw_in[c], 16)

            sp.dma_start(packw_f[:, :], packw_in).then_inc(const_in, 16)
            load_half(0, 0)
            load_half(0, 1)
            sp.dma_start(resid[:, :, :], x_rows).then_inc(x_in, 16)
            sp.dma_start(ident[:, :], ident_in).then_inc(const_in, 16)
            sp.dma_start(w0_sb[:, :], w0).then_inc(const_in, 16)
            sp.dma_start(w1_sb[:, :], w1).then_inc(const_in, 16)
            load_half(0, 2)
            load_half(0, 3)
            with sp.Fori(1, NPAIR) as t:
                for c in range(SLOTS):
                    sp.wait_ge(half_packed, SLOTS * t + (c + 1 - SLOTS))
                    sp.wait_ge(half_checked, SLOTS * t + (c + 1 - SLOTS))
                    load_half(t, c)

            def store_pair(v):
                sp.dma_start(out_rows[:, ds(2 * v, 2), :], x1[:, :, :]).then_inc(out_written, 16)

            with sp.Fori(0, NPAIR) as v:
                sp.wait_ge(normed, v + (NPAIR + 1))
                store_pair(v)
            sp.wait_ge(out_written, 16 * NPAIR)

            sp.wait_ge(flag_ready, 1)
            taken = sp.value_load(flag[0:1, 0:1], min_val=0, max_val=1)
            with sp.If(taken != 0):
                sp.dma_start(g_x, x_rows).then_inc(g_x_in, 16)
                for layer in range(2):
                    with sp.Fori(0, NB) as i:
                        with sp.Fori(0, GN) as c:
                            n = i * GN + c + layer * NB * GN
                            sp.wait_ge(g_chunk_free, n + 1)
                            sp.wait_ge(g_row_summed, n + 1)
                            sp.dma_start(g_chunk, adj_stripes[:, ds(i, 1), ds(c * GCH, GCH)]
                                         .rearrange("p a n -> p (a n)")).then_inc(g_chunk_in, 16)
                        if layer == 1:
                            sp.wait_ge(g_rows_ready, i + 1)
                            sp.dma_start(out_rows[:, ds(i, 1), :].rearrange("p a f -> p (a f)"), x1[:, 0, :])\
                              .then_inc(g_out, 16)
                sp.wait_ge(g_out, 16 * NB)

        @block.tensor
        def _(pe):
            raw_hi = [r[:, :].bitcast(bf16) for r in raw]
            blocks = [spread[:, s, :, :, :].rearrange("p j s c -> p (j s c)").bitcast(fp8) for s in range(2)]

            def pack(t, s):
                if not isinstance(t, int) or t > 0:
                    pe.wait_ge(words_copied, 2 * t + (s - 1))
                for half in range(2):
                    c = 2 * s + half
                    pe.wait_ge(raw_in[c], 16 * t + 16)
                    for b in range(HB):
                        j = half * HB + b
                        last = nc.tensor.matmul(ps_words[s][:, j * WPB:(j + 1) * WPB],
                                                raw_hi[c][:, 2 * P * b + 1:2 * P * (b + 1):2], packw[:, :],
                                                start=True, stop=True)
                    last.then_inc(half_packed, 1)

            def product(t, s, known):
                pe.wait_ge(spread_done, 2 * t + (s + 1))
                if not isinstance(t, int) or t > 0:
                    pe.wait_ge(agg_read, 2 * t + (s - 1))
                apart(pe)
                for j in range(NB):
                    w = XW + ZW if j < known else XW
                    last = nc.tensor.matmul(ps_agg[s][:, 0:w], blocks[s][:, j * P:(j + 1) * P], xz[:, j, 0:w],
                                            start=(j == 0), stop=(j == NB - 1))
                last.then_inc(product_done, 1)

            def product2(t, s, known, lo, hi):
                if lo == known:
                    pe.wait_ge(spread_done, 2 * t + (s + 1 + NB))
                    pe.wait_ge(agg_read, 2 * t + (s - 1 + NB))
                apart(pe)
                for j in range(lo, hi):
                    last = nc.tensor.matmul(ps_agg[s][:, 0:ZW], blocks[s][:, j * P:(j + 1) * P],
                                            xz[:, j, XW:XW + ZW], start=(j == known), stop=(j == NB - 1))
                if hi == NB:
                    last.then_inc(product_done, 1)

            def transpose_cat(w):
                pe.wait_ge(cat_written, w + 1)
                for s in range(2):
                    last = nc.tensor.transpose(ps_catT[:, s * P:(s + 1) * P], cat[:, s, :], ident[:, :])
                last.then_inc(cat_transposed, 1)

            def linear0(w):
                pe.wait_ge(catT_copied, w + 1)
                for s in range(2):
                    last = nc.tensor.matmul(ps_lin0[:, s * D:(s + 1) * D], catT[:, s * P:(s + 1) * P], w0T[:, :],
                                            start=True, stop=True)
                last.then_inc(lin0_done, 1)

            def transpose_x1(w):
                pe.wait_ge(normed, w + 1)
                apart(pe)
                for s in range(2):
                    last = nc.tensor.transpose(ps_x1T[0:D, s * P:(s + 1) * P], x1[:, s, :], ident[:, :])
                last.then_inc(x1_transposed, 1)

            def linear1(w):
                pe.wait_ge(x1T_copied, w + 1)
                for s in range(2):
                    last = nc.tensor.matmul(ps_z[:, s * D:(s + 1) * D], x1T[:, s * P:(s + 1) * P], w1_sb[:, :],
                                            start=True, stop=True)
                last.then_inc(z_done, 1)

            def pair_body(v, known):
                transpose_x1(v - 2)
                pack(v, 1)
                linear1(v - 2)
                product(v, 0, known)
                transpose_cat(v - 1)
                pack(v + 1, 0)
                linear0(v - 1)
                product(v, 1, known)

            pe.wait_ge(consts_made, 3)
            pack(0, 0)
            pack(0, 1)
            pe.wait_ge(const_in, 16 * 4)
            nc.tensor.transpose(ps_x1T[:, 0:D], w0_sb[:, :], ident[0:D, 0:D]).then_inc(w0_transposed, 1)
            pe.wait_ge(w0T_copied, 1)
            pe.wait_ge(x_split, 2)
            product(0, 0, 0)
            pack(1, 0)
            product(0, 1, 0)
            pack(1, 1)
            product(1, 0, 0)
            transpose_cat(0)
            pack(2, 0)
            linear0(0)
            product(1, 1, 0)
            for g in range(GROUPS):
                if g > 0:
                    pe.wait_ge(z_stored, KNOWN[g] // 2)
                with pe.Fori(max(2, g * PPG), min((g + 1) * PPG, NPAIR - 1)) as v:
                    pair_body(v, KNOWN[g])
            v, known = NPAIR - 1, KNOWN[GROUPS - 1]
            transpose_x1(v - 2)
            pack(v, 1)
            linear1(v - 2)
            product(v, 0, known)
            transpose_cat(v - 1)
            linear0(v - 1)
            product(v, 1, known)

            transpose_x1(v - 1)
            linear1(v - 1)
            product2(0, 0, 0, 0, NB // 2)
            transpose_cat(v)
            linear0(v)
            product2(0, 0, 0, NB // 2, NB - LAG)
            transpose_x1(v)
            linear1(v)
            pe.wait_ge(z_stored, NPAIR)
            product2(0, 0, 0, NB - LAG, NB)
            product2(0, 1, 0, 0, NB)
            pe.wait_ge(bad_counted, 1)
            nc.tensor.matmul(ps_lin0[0:1, 0:1], bad_row[:, :], ones[:, :], start=True, stop=True)\
              .then_inc(bad_summed, 1)
            for g in range(GROUPS):
                with pe.Fori(max(1, g * PPG), (g + 1) * PPG) as v:
                    for s in range(2):
                        product2(v, s, KNOWN[g], KNOWN[g], NB)

            pe.wait_ge(flag_ready, 1)
            taken = pe.value_load(flag[0:1, 0:1], min_val=0, max_val=1)
            with pe.If(taken != 0):
                pe.wait_ge(out_written, 16 * NPAIR)
                pe.wait_ge(g_x_in, 16)
                pe.sem_inc(g_chunk_free, 1)
                for layer, source in enumerate((g_x, g_z)):
                    with pe.Fori(0, NB) as i:
                        with pe.Fori(0, GN) as c:
                            n = i * GN + c + layer * NB * GN
                            pe.wait_ge(g_chunk_in, 16 * n + 16)
                            pe.wait_ge(g_added, n + 1)
                            for q in range(GQ):
                                last = nc.tensor.transpose(ps_words[0][:, q * P:(q + 1) * P],
                                                           g_chunk[:, q * P:(q + 1) * P], ident[:, :])
                            last.then_inc(g_chunk_free, 1)
                            pe.wait_ge(g_copied, n + 1)
                            for q in range(GQ):
                                last = nc.tensor.matmul(ps_agg[0][:, 0:D], g_chunkT[:, q * P:(q + 1) * P],
                                                        source[:, ds(c * GQ + q, 1), :].rearrange("p a f -> p (a f)"),
                                                        start=(q == 0), stop=(q == GQ - 1))
                            last.then_inc(g_partial, 1)
                        if layer == 0:
                            pe.wait_ge(g_dve, 3 * i + 2)
                            nc.tensor.transpose(ps_catT[:, 0:P], cat[:, 0, :], ident[:, :]).then_inc(g_pe, 1)
                            pe.wait_ge(g_act, 4 * i + 1)
                            nc.tensor.matmul(ps_lin0[:, 0:D], catT[:, 0:P], w0T[:, :], start=True, stop=True)\
                              .then_inc(g_pe, 1)
                            pe.wait_ge(g_dve, 3 * i + 4)
                            apart(pe)
                            nc.tensor.transpose(ps_x1T[0:D, 0:P], x1[:, 0, :], ident[:, :]).then_inc(g_pe, 1)
                            pe.wait_ge(g_act, 4 * i + 3)
                            nc.tensor.matmul(ps_z[:, 0:D], x1T[:, 0:P], w1_sb[:, :], start=True, stop=True)\
                              .then_inc(g_pe, 1)
                    if layer == 0:
                        pe.wait_ge(g_rows_ready, 1)

        @block.scalar
        def _(act):
            def copy_words(t, s, g):
                stripe_in_group = 2 * t + (s - SPG * g)
                act.wait_ge(half_packed, 4 * t + (2 * s + 2))
                if not isinstance(t, int) or t > 0:
                    act.wait_ge(spread_done, 2 * t + (s - 1))
                nc.scalar.activation(words_now[:, s, :], ps_words[s][:, :], ACT.Copy)
                nc.scalar.activation(words[g][:, ds(stripe_in_group, 1), :].rearrange("p a b -> p (a b)"),
                                     ps_words[s][:, KNOWN[g] * WPB:NB * WPB], ACT.Copy).then_inc(words_copied, 1)

            def copy_catT(w):
                act.wait_ge(cat_transposed, w + 1)
                nc.scalar.activation(catT[:, :], ps_catT[:, 0:2 * P], ACT.Copy).then_inc(catT_copied, 1)

            def copy_x1T(w):
                act.wait_ge(x1_transposed, w + 1)
                nc.scalar.activation(x1T[:, :], ps_x1T[0:D, 0:2 * P], ACT.Copy).then_inc(x1T_copied, 1)

            def standard_deviation(n, eps):
                act.wait_ge(var_ready, n + 1)
                nc.scalar.activation(std[:, :], meanvar[:, :, 1], ACT.Sqrt, bias=eps[:, :]).then_inc(std_ready, 1)

            def store_z_hi(w):
                act.wait_ge(z_done, w + 1)
                nc.scalar.activation(xz[:, ds(2 * w, 2), XW:XW + D], ps_z_v, ACT.Copy).then_inc(z_hi_stored, 1)

            def pair_body(u, g):
                copy_catT(u - 2)
                copy_words(u, 0, g)
                standard_deviation(u - 2, eps1)
                copy_x1T(u - 2)
                copy_words(u, 1, g)
                store_z_hi(u - 2)

            act.wait_ge(consts_made, 3)
            copy_words(0, 0, 0)
            act.wait_ge(x_in, 16)
            for q in range(2):
                nc.scalar.activation(xz[:, q * QX:(q + 1) * QX, 0:D], resid[:, q * QX:(q + 1) * QX, :], ACT.Copy)\
                  .then_inc(x_hi_stored, 1)
            for q in range(2):
                act.wait_ge(x_rest_made, q + 1)
                nc.scalar.activation(xz[:, q * QX:(q + 1) * QX, D:2 * D], x_rest[q], ACT.Copy)\
                  .then_inc(x_mid_stored, 1)
            copy_words(0, 1, 0)
            act.wait_ge(w0_transposed, 1)
            nc.scalar.activation(w0T[:, :], ps_x1T[:, 0:D], ACT.Copy).then_inc(w0T_copied, 1)
            copy_words(1, 0, 0)
            copy_words(1, 1, 0)
            for g in range(GROUPS):
                with act.Fori(max(2, g * PPG), (g + 1) * PPG) as u:
                    pair_body(u, g)
            w = NPAIR - 2
            copy_catT(w)
            standard_deviation(w, eps1)
            copy_x1T(w)
            store_z_hi(w)
            copy_catT(w + 1)
            standard_deviation(w + 1, eps1)
            copy_x1T(w + 1)
            store_z_hi(w + 1)
            with act.Fori(0, NPAIR) as v:
                standard_deviation(v + NPAIR, eps4)

            act.wait_ge(flag_ready, 1)
            taken = act.value_load(flag[0:1, 0:1], min_val=0, max_val=1)
            with act.If(taken != 0):
                act.wait_ge(out_written, 16 * NPAIR)
                for layer in range(2):
                    with act.Fori(0, NB) as i:
                        with act.Fori(0, GN) as c:
                            n = i * GN + c + layer * NB * GN
                            act.wait_ge(g_chunk_free, n + 2)
                            nc.scalar.activation(g_chunkT, ps_words[0][:, :], ACT.Copy).then_inc(g_copied, 1)
                        if layer == 0:
                            act.wait_ge(g_pe, 4 * i + 1)
                            nc.scalar.activation(catT[:, 0:P], ps_catT[:, 0:P], ACT.Copy).then_inc(g_act, 1)
                            act.wait_ge(g_dve, 3 * i + 3)
                            nc.scalar.activation(std[:, 0:1], meanvar[:, 0, 1:2], ACT.Sqrt, bias=eps1[:, :])\
                              .then_inc(g_act, 1)
                            act.wait_ge(g_pe, 4 * i + 3)
                            nc.scalar.activation(x1T[:, 0:P], ps_x1T[0:D, 0:P], ACT.Copy).then_inc(g_act, 1)
                            act.wait_ge(g_pe, 4 * i + 4)
                            nc.scalar.activation(g_z[:, ds(i, 1), :].rearrange("p a f -> p (a f)"), ps_z[:, 0:D],
                                                 ACT.Copy).then_inc(g_act, 1)
                        else:
                            act.wait_ge(g_dve, i + (3 * NB + 2))
                            nc.scalar.activation(std[:, 0:1], meanvar[:, 0, 1:2], ACT.Sqrt, bias=eps1[:, :])\
                              .then_inc(g_act, 1)

        @block.vector
        def _(dve):
            now_lanes = [words_now[:, s, :].bitcast(u32).rearrange("p (j c) -> p j c", c=UPB) for s in range(2)]

            def check(t, s, half):
                c = 2 * s + half
                dve.wait_ge(raw_in[c], 16 * t + 16)
                if not isinstance(t, int) or 4 * t + c > 0:
                    dve.wait_ge(half_checked, 4 * t + c)
                nc.vector.scalar_tensor_tensor(verdict[:, :], raw[c][:, :], 0.0, raw[c][:, :], ALU.is_gt, ALU.not_equal,
                                               accum_out=bad[:, ds(4 * t + c, 1)]).then_inc(half_checked, 1)

            def spread_bits(s, lanes, first):
                for k in range(SHIFTS):
                    op = ALU.logical_shift_left if k <= TWO_FP8 else ALU.logical_shift_right
                    last = nc.vector.tensor_scalar(spread[:, s, first:NB, k, :], lanes, abs(TWO_FP8 - k), TWO_MASK,
                                                   op, ALU.bitwise_and)
                last.then_inc(spread_done, 1)

            def spread_now(t, s):
                dve.wait_ge(words_copied, 2 * t + (s + 1))
                if not isinstance(t, int) or t > 0:
                    dve.wait_ge(product_done, 2 * t + (s - 1))
                spread_bits(s, now_lanes[s], 0)

            def spread_kept(v, s, g):
                dve.wait_ge(product_done, 2 * v + (s - 1 + NB))
                kept = words[g][:, ds(2 * v + (s - SPG * g), 1), :].rearrange("p a b -> p (a b)")\
                    .bitcast(u32).rearrange("p (j c) -> p j c", c=UPB)
                spread_bits(s, kept, KNOWN[g])

            def read_sums(w, s, with_z):
                dve.wait_ge(product_done, 2 * w + (s + 1))
                if s == 0 and (not isinstance(w, int) or w > 0):
                    dve.wait_ge(cat_written, w)
                nc.vector.tensor_reduce(agg[:, s, :], ps_agg[s][:, 0:3 * D].rearrange("p (k f) -> p f k", k=3),
                                        axis=AX, op=ALU.add)
                if with_z:
                    nc.vector.tensor_reduce(part[:, s, :], ps_agg[s][:, XW:XW + ZW].rearrange("p (k f) -> p f k", k=3),
                                            axis=AX, op=ALU.add)
                nc.vector.tensor_scalar(deg[:, s:s + 1], ps_agg[s][:, 3 * D:3 * D + 1], 2.0, None, ALU.max)\
                  .then_inc(agg_read, 1)

            def invert_degree(w):
                dve.wait_ge(agg_read, 2 * w + 2)
                nc.vector.reciprocal(deg_inv[:, :], deg[:, :]).then_inc(deg_inverted, 1)

            def moments(n):
                dve.wait_ge(h_written, n + 1)
                for s in range(2):
                    last = nc.vector.bn_stats(stats[:, s, :], h[:, s, :])
                last.then_inc(stats_written, 1)
                dve.wait_ge(stats_written, n + 1)
                apart(dve)
                for s in range(2):
                    last = nc.vector.bn_aggr(meanvar[:, s, :], stats[:, s, :])
                last.then_inc(var_ready, 1)

            def residual1(w):
                dve.wait_ge(lin0_done, w + 1)
                nc.vector.scalar_tensor_tensor(h[:, :, :], ps_lin0_v, 0.0, resid[:, ds(2 * w, 2), :], ALU.max, ALU.add)\
                  .then_inc(h_written, 1)
                moments(w)

            def invert_std(n):
                dve.wait_ge(std_ready, n + 1)
                nc.vector.reciprocal(rstd[:, :], std[:, :]).then_inc(rstd_ready, 1)

            def z_minus_hi(w):
                dve.wait_ge(z_hi_stored, w + 1)
                nc.vector.tensor_tensor(z_rest[:, :, :], ps_z_v, xz[:, ds(2 * w, 2), XW:XW + D], ALU.subtract)\
                  .then_inc(z_rest_made, 1)

            def pair_body(u, with_z):
                for half in range(2):
                    check(u, 0, half)
                residual1(u - 2)
                spread_now(u, 0)
                invert_std(u - 2)
                read_sums(u - 1, 0, with_z)
                for half in range(2):
                    check(u, 1, half)
                z_minus_hi(u - 2)
                spread_now(u, 1)
                read_sums(u - 1, 1, with_z)
                invert_degree(u - 1)

            nc.vector.memset(ones[:, :], 1.0)
            nc.vector.memset(eps1[:, :], EPS).then_inc(consts_made, 1)
            nc.vector.memset(eps4[:, :], 4 * EPS).then_inc(consts_made, 1)
            nc.vector.memset(xz[:, :, 3 * D:3 * D + 1], 1.0)
            dve.wait_ge(const_in, 16 * 4)
            nc.vector.tensor_copy(packw[:, :], packw_f[:, :]).then_inc(consts_made, 1)
            for half in range(2):
                check(0, 0, half)
            spread_now(0, 0)
            for q in range(2):
                dve.wait_ge(x_hi_stored, q + 1)
                nc.vector.tensor_tensor(x_rest[q], resid[:, q * QX:(q + 1) * QX, :], xz[:, q * QX:(q + 1) * QX, 0:D],
                                        ALU.subtract).then_inc(x_rest_made, 1)
            for q in range(2):
                dve.wait_ge(x_mid_stored, q + 1)
                nc.vector.tensor_tensor(xz[:, q * QX:(q + 1) * QX, 2 * D:3 * D], x_rest[q],
                                        xz[:, q * QX:(q + 1) * QX, D:2 * D], ALU.subtract).then_inc(x_split, 1)
            for half in range(2):
                check(0, 1, half)
            spread_now(0, 1)
            for half in range(2):
                check(1, 0, half)
            spread_now(1, 0)
            read_sums(0, 0, False)
            for half in range(2):
                check(1, 1, half)
            spread_now(1, 1)
            read_sums(0, 1, False)
            invert_degree(0)
            with dve.Fori(2, PPG + 1) as u:
                pair_body(u, False)
            with dve.Fori(PPG + 1, NPAIR) as u:
                pair_body(u, True)
            w = NPAIR - 2
            dve.wait_ge(half_checked, 4 * NPAIR)
            nc.vector.tensor_reduce(bad_row[:, :], bad[:, :], axis=AX, op=ALU.add).then_inc(bad_counted, 1)
            residual1(w)
            spread_kept(0, 0, 0)
            invert_std(w)
            read_sums(w + 1, 0, True)
            spread_kept(0, 1, 0)
            z_minus_hi(w)
            read_sums(w + 1, 1, True)
            invert_degree(w + 1)
            residual1(w + 1)
            invert_std(w + 1)
            z_minus_hi(w + 1)

            def read_sums2(v, s):
                dve.wait_ge(product_done, 2 * v + (s + 1 + NB))
                nc.vector.tensor_reduce(agg[:, s, :], ps_agg[s][:, 0:ZW].rearrange("p (k f) -> p f k", k=3),
                                        axis=AX, op=ALU.add).then_inc(agg_read, 1)

            def residual2(v):
                dve.wait_ge(agg_read, 2 * v + (2 + NB))
                dve.wait_ge(normed, v + NPAIR)
                nc.vector.tensor_tensor(h[:, :, :], agg[:, :, :], resid[:, ds(2 * v, 2), :], ALU.add)\
                  .then_inc(h_written, 1)
                moments(v + NPAIR)

            def pair_body2(v, g):
                spread_kept(v, 0, g)
                read_sums2(v - 1, 0)
                spread_kept(v, 1, g)
                read_sums2(v - 1, 1)
                residual2(v - 1)
                invert_std(v - 1 + NPAIR)

            dve.wait_ge(resid_written, NPAIR)
            for g in range(GROUPS):
                with dve.Fori(max(1, g * PPG), (g + 1) * PPG) as v:
                    pair_body2(v, g)
            read_sums2(NPAIR - 1, 0)
            read_sums2(NPAIR - 1, 1)
            dve.wait_ge(bad_summed, 1)
            nc.vector.tensor_scalar(flag[:, :], ps_lin0[0:1, 0:1], 0.0, None, ALU.is_gt).then_inc(flag_ready, 1)
            residual2(NPAIR - 1)
            invert_std(2 * NPAIR - 1)

            dve.wait_ge(flag_ready, 1)
            taken = dve.value_load(flag[0:1, 0:1], min_val=0, max_val=1)
            with dve.If(taken != 0):
                dve.wait_ge(out_written, 16 * NPAIR)
                dve.wait_ge(g_x_in, 16)
                dve.sem_inc(g_row_summed, 1)
                dve.sem_inc(g_added, 1)
                nc.vector.memset(deg_inv[:, :], 0.0).then_inc(g_dve, 1)

                def g_normalise(rows, m):
                    nc.vector.bn_stats(stats[:, 0, :], h[:, 0, :]).then_inc(stats_written, 1)
                    dve.drain()
                    nc.vector.bn_aggr(meanvar[:, 0, :], stats[:, 0, :]).then_inc(g_dve, 1)
                    dve.wait_ge(g_act, m)
                    nc.vector.reciprocal(rstd[:, 0:1], std[:, 0:1])
                    dve.drain()
                    return nc.vector.tensor_scalar(rows, h[:, 0, :], meanvar[:, 0, 0:1], rstd[:, 0:1],
                                                   ALU.subtract, ALU.mult)

                for layer in range(2):
                    with dve.Fori(0, NB) as i:
                        nc.vector.memset(g_acc, 0.0)
                        nc.vector.memset(deg[:, 0:1], 0.0)
                        dve.drain()
                        with dve.Fori(0, GN) as c:
                            n = i * GN + c + layer * NB * GN
                            dve.wait_ge(g_chunk_in, 16 * n + 16)
                            nc.vector.tensor_reduce(g_rowsum, g_chunk, axis=AX, op=ALU.add).then_inc(g_row_summed, 1)
                            dve.drain()
                            nc.vector.tensor_tensor(deg[:, 0:1], deg[:, 0:1], g_rowsum, ALU.add)
                            dve.wait_ge(g_partial, n + 1)
                            nc.vector.tensor_tensor(g_acc, g_acc, ps_agg[0][:, 0:D], ALU.add).then_inc(g_added, 1)
                            dve.drain()
                        if layer == 0:
                            nc.vector.tensor_scalar(deg[:, 1:2], deg[:, 0:1], 1.0, None, ALU.max)
                            dve.drain()
                            nc.vector.reciprocal(deg_inv[:, 0:1], deg[:, 1:2])
                            nc.vector.tensor_copy(cat[:, 0, 0:D], g_x[:, ds(i, 1), :].rearrange("p a f -> p (a f)"))
                            dve.drain()
                            nc.vector.tensor_scalar(cat[:, 0, D:2 * D], g_acc, deg_inv[:, 0:1], None, ALU.mult)\
                              .then_inc(g_dve, 1)
                            dve.wait_ge(g_pe, 4 * i + 2)
                            nc.vector.scalar_tensor_tensor(h[:, 0, :], ps_lin0[:, 0:D], 0.0,
                                                           g_x[:, ds(i, 1), :].rearrange("p a f -> p (a f)"),
                                                           ALU.max, ALU.add)
                            dve.drain()
                            g_normalise(x1[:, 0, :], 4 * i + 2).then_inc(g_dve, 1)
                            dve.drain()
                            nc.vector.tensor_copy(g_x1[:, ds(i, 1), :].rearrange("p a f -> p (a f)"), x1[:, 0, :])
                            dve.wait_ge(g_act, 4 * i + 4)
                        else:
                            nc.vector.tensor_tensor(h[:, 0, :], g_acc,
                                                    g_x1[:, ds(i, 1), :].rearrange("p a f -> p (a f)"), ALU.add)
                            dve.drain()
                            g_normalise(x1_twice[:, 0, :], i + (4 * NB + 1))
                            dve.drain()
                            nc.vector.tensor_copy(x1[:, 0, :], x1_twice[:, 0, :]).then_inc(g_rows_ready, 1)
                    if layer == 0:
                        nc.vector.memset(x1[:, 1, :], 0.0).then_inc(g_rows_ready, 1)

        @block.gpsimd
        def _(pool):
            def write_cat(w, with_z):
                pool.wait_ge(deg_inverted, w + 1)
                if not isinstance(w, int) or w > 0:
                    pool.wait_ge(cat_transposed, w)
                apart(pool)
                if with_z:
                    nc.gpsimd.tensor_copy(part_kept[:, :, :], part[:, :, :])
                nc.gpsimd.tensor_copy(cat[:, :, 0:D], resid[:, ds(2 * w, 2), :])
                nc.gpsimd.tensor_tensor(cat[:, :, D:2 * D], agg[:, :, :],
                                        deg_inv[:, :].unsqueeze(2).to_broadcast([P, 2, D]), ALU.mult)\
                  .then_inc(cat_written, 1)

            def normalise(n):
                pool.wait_ge(rstd_ready, n + 1)
                apart(pool)
                for s in range(2):
                    last = nc.gpsimd.tensor_scalar(x1[:, s, :], h[:, s, :], meanvar[:, s, 0:1], rstd[:, s:s + 1],
                                                   ALU.subtract, ALU.mult)
                last.then_inc(normed, 1)

            def keep_x1(w, with_z):
                normalise(w)
                pool.wait_ge(normed, w + 1)
                apart(pool)
                if with_z:
                    nc.gpsimd.tensor_tensor(x1_twice[:, :, :], x1[:, :, :], x1[:, :, :], ALU.add)\
                      .then_inc(x1_doubled, 1)
                    pool.wait_ge(x1_doubled, w - (PPG - 1))
                    apart(pool)
                    nc.gpsimd.tensor_tensor(resid[:, ds(2 * w, 2), :], x1_twice[:, :, :], part_kept[:, :, :], ALU.add)\
                      .then_inc(resid_written, 1)
                else:
                    nc.gpsimd.tensor_tensor(resid[:, ds(2 * w, 2), :], x1[:, :, :], x1[:, :, :], ALU.add)\
                      .then_inc(resid_written, 1)

            def store_z(w):
                pool.wait_ge(z_rest_made, w + 1)
                apart(pool)
                nc.gpsimd.tensor_copy(xz[:, ds(2 * w, 2), XW + D:XW + 2 * D], z_rest[:, :, :])\
                  .then_inc(z_mid_stored, 1)
                pool.wait_ge(z_mid_stored, w + 1)
                apart(pool)
                nc.gpsimd.tensor_tensor(xz[:, ds(2 * w, 2), XW + 2 * D:XW + 3 * D], z_rest[:, :, :],
                                        xz[:, ds(2 * w, 2), XW + D:XW + 2 * D], ALU.subtract).then_inc(z_stored, 1)

            write_cat(0, False)
            with pool.Fori(2, PPG + 1) as u:
                keep_x1(u - 2, False)
                store_z(u - 2)
                write_cat(u - 1, False)
            keep_x1(PPG - 1, False)
            store_z(PPG - 1)
            write_cat(PPG, True)
            with pool.Fori(PPG + 2, NPAIR + 1) as u:
                keep_x1(u - 2, True)
                store_z(u - 2)
                write_cat(u - 1, True)
            keep_x1(NPAIR - 1, True)
            store_z(NPAIR - 1)

            pool.wait_ge(x1_transposed, NPAIR)
            normalise(NPAIR)
            with pool.Fori(1, NPAIR) as v:
                pool.wait_ge(out_written, 16 * v)
                normalise(v + NPAIR)


_INS = ['x', 'adj', 'L0_gnn_W', 'L1_gnn_weight']


def kernel(**inputs):
    import numpy as _np
    import concourse.bacc as _bacc
    from concourse import mybir as _mybir
    from concourse.bass_utils import run_bass_kernel_spmd as _run

    nc = _bacc.Bacc("TRN2", target_bir_lowering=False, num_devices=1)
    arrays, args = {}, []
    named = [(name, _np.ascontiguousarray(inputs[name])) for name in _INS]
    named += [("pack_weights", pack_weights()), ("identity", _np.eye(P, dtype=_np.float32))]
    for name, a in named:
        arrays[f"in_{name}_dram"] = a
        args.append(nc.dram_tensor(f"in_{name}_dram", a.shape, _mybir.dt.from_np(a.dtype), kind="ExternalInput").ap())
    args.append(nc.dram_tensor("out_0_dram", (N, D), _mybir.dt.float32, kind="ExternalOutput").ap())
    gnn_kernel(nc, *args)
    r = _run(nc, [arrays], core_ids=[0])
    return r.results[0]["out_0_dram"]
```

```python
from contextlib import ExitStack

import numpy as np
import concourse.bass as bass
from concourse import mybir

P = 128
N = 8192
D = 64
NB = N // P
NPAIR = NB // 2
EPS = 1e-5

HALF = N // 2
HB = NB // 2
SLOTS = 4

ACOLS = 1024
ONE_HI = 0x3F80
DOWN = 64

BITS = 16
WPB = P // BITS
PACKN = 64
UPB = WPB // 2
SHIFTS = 8
TWO_FP8 = 6
TWO_MASK = 0x40404040

GROUPS = 4
PPG = NPAIR // GROUPS
SPG = NB // GROUPS
LAG = 4
KNOWN = [max(0, SPG * g - LAG) for g in range(GROUPS)]

LATE = max(KNOWN[g + 1] - KNOWN[g] for g in range(GROUPS - 1))
LATE_BEFORE = [PPG * g * (g - 1) // 2 for g in range(GROUPS + 1)]
LAST = KNOWN[GROUPS - 1]

XW = 3 * D + 1
ZW = 3 * D
XZ = XW + ZW + 1

GCH = 512
GQ = GCH // P
GN = N // GCH


def pack_weights():
    w = np.zeros((P, PACKN), np.float32)
    for i in range(P):
        w[i, (i % BITS) // 2] = 2.0 ** (8 * (i % 2) + i // BITS)
    return w


def gnn_kernel(nc, x, adj, w0, w1, packw_in, ident_in, out):
    fp32, bf16, u8 = mybir.dt.float32, mybir.dt.bfloat16, mybir.dt.uint8
    u16, u32, i32, fp8 = mybir.dt.uint16, mybir.dt.uint32, mybir.dt.int32, mybir.dt.float8e4
    ALU = mybir.AluOpType
    ACT = mybir.ActivationFunctionType
    AX = mybir.AxisListType.X
    ds = bass.ds

    ctx = ExitStack()
    with ctx:
        def sb(name, shape, dt):
            return ctx.enter_context(nc.sbuf_tensor(name, shape, dt))

        def pb(name, shape, dt):
            return ctx.enter_context(nc.psum_tensor(name, shape, dt))

        def sem(name):
            return ctx.enter_context(nc.semaphore(name))

        raw = [sb(f"raw{c}", [P, HALF], fp32) for c in range(SLOTS)]
        words = [sb(f"words{g}", [P, SPG, (NB - KNOWN[g]) * WPB], u16) for g in range(GROUPS)]
        words_now = sb("words_now", [P, NB * WPB], u16)
        spread = sb("spread", [P, 2, NB, SHIFTS, UPB], u32)
        xz = sb("xz", [P, NB, XZ], bf16)
        resid = sb("resid", [P, NB, D], fp32)
        verdict = sb("verdict", [P, HALF - ACOLS + 3 * ACOLS], u8)
        above_one = sb("above_one", [P, 2 * NB], fp32)
        from_middle = sb("from_middle", [P, 2 * NB], fp32)
        low_bits = sb("low_bits", [P, 2 * NB], fp32)
        minus_one_hi = sb("minus_one_hi", [P, 1], fp32)
        minus_middle = sb("minus_middle", [P, 1], fp32)
        bad = sb("bad", [P, 2 * NB], fp32)
        bad_row = sb("bad_row", [P, 1], fp32)
        flag = sb("flag", [1, 1], i32)
        ident = sb("ident", [P, P], fp32)
        packw = sb("packw", [P, PACKN], bf16)
        ones = sb("ones", [P, 1], fp32)
        eps1 = sb("eps1", [P, 1], fp32)
        eps4 = sb("eps4", [P, 1], fp32)
        w0T = sb("w0T", [2 * D, D], fp32)
        w1_sb = sb("w1_sb", [D, D], fp32)
        agg = sb("agg", [P, 2, D], fp32)
        part = sb("part", [P, 2, D], fp32)
        late = sb("late", [P, 2, LATE, SHIFTS, UPB], u32)
        late_sum = sb("late_sum", [P, 2, D], fp32)
        part_kept = sb("part_kept", [P, 2, D], fp32)
        deg = sb("deg", [P, 2], fp32)
        deg_inv = sb("deg_inv", [P, 2], fp32)
        cat = sb("cat", [P, 2, 2 * D], fp32)
        w0_sb = cat[0:D, 0, :]
        catT = sb("catT", [2 * D, 2 * P], fp32)
        stats = sb("stats", [P, 2, 6], fp32)
        meanvar = sb("meanvar", [P, 2, 2, 2], fp32)
        std = sb("std", [P, 2, 2], fp32)
        rstd = sb("rstd", [P, 2, 2], fp32)
        x1 = sb("x1", [P, 2, D], fp32)
        x1_twice = sb("x1_twice", [P, 2, D], fp32)
        h = [sb("h0", [P, 2, D], fp32), x1_twice]
        x1T = catT[0:D, :]
        z_rest = sb("z_rest", [P, 2, D], fp32)
        packw_f = z_rest[:, :, :].rearrange("p a f -> p (a f)")[:, 0:PACKN]

        ps_words = [pb(f"ps_words{i}", [P, 512], fp32) for i in range(2)]
        ps_agg = pb("ps_agg", [P, 2, 512], fp32)
        ps_late = pb("ps_late", [P, 2, 512], fp32)
        ps_transposed = pb("ps_transposed", [P, 512], fp32)
        ps_linear = pb("ps_linear", [P, 512], fp32)
        ps_linear_v = ps_linear[:, 0:2 * D].rearrange("p (a f) -> p a f", a=2)

        QX = NB // 2
        x_rest = [words[1 + q][:, :, :].rearrange("p a b -> p (a b)")[:, 0:QX * D * 2].bitcast(fp32)
                  .rearrange("p (j f) -> p j f", f=D) for q in range(2)]

        raw_in = [sem(f"raw_in{c}") for c in range(SLOTS)]
        x_in = sem("x_in")
        const_in = sem("const_in")
        out_written = sem("out_written")
        consts_made = sem("consts_made")
        w0_transposed = sem("w0_transposed")
        w0T_copied = sem("w0T_copied")
        x_hi_stored = sem("x_hi_stored")
        x_rest_made = sem("x_rest_made")
        x_mid_stored = sem("x_mid_stored")
        x_split = sem("x_split")
        half_packed = sem("half_packed")
        half_checked = sem("half_checked")
        half_checked_act = sem("half_checked_act")
        bad_listed = sem("bad_listed")
        words_copied = sem("words_copied")
        spread_done = sem("spread_done")
        product_done = sem("product_done")
        agg_read = sem("agg_read")
        late_spread = sem("late_spread")
        late_product = sem("late_product")
        late_read = sem("late_read")
        late_added = sem("late_added")
        last_spread = sem("last_spread")
        last_product = sem("last_product")
        last_read = sem("last_read")
        centred = sem("centred")
        deg_inverted = sem("deg_inverted")
        cat_written = sem("cat_written")
        cat_transposed = sem("cat_transposed")
        catT_copied = sem("catT_copied")
        lin0_done = sem("lin0_done")
        h_written = sem("h_written")
        stats_written = sem("stats_written")
        var_ready = sem("var_ready")
        std_ready = sem("std_ready")
        rstd_ready = sem("rstd_ready")
        normed = sem("normed")
        x1_doubled = sem("x1_doubled")
        resid_written = sem("resid_written")
        x1_transposed = sem("x1_transposed")
        x1T_copied = sem("x1T_copied")
        z_done = sem("z_done")
        z_hi_stored = sem("z_hi_stored")
        z_rest_made = sem("z_rest_made")
        z_mid_stored = sem("z_mid_stored")
        z_stored = sem("z_stored")
        bad_counted = sem("bad_counted")
        bad_summed = sem("bad_summed")
        flag_ready = sem("flag_ready")
        g_x_in = sem("g_x_in")
        g_chunk_in = sem("g_chunk_in")
        g_chunk_free = sem("g_chunk_free")
        g_row_summed = sem("g_row_summed")
        g_transposed = sem("g_transposed")
        g_copied = sem("g_copied")
        g_partial = sem("g_partial")
        g_added = sem("g_added")
        g_dve = sem("g_dve")
        g_rows_ready = sem("g_rows_ready")
        g_pe = sem("g_pe")
        g_act = sem("g_act")
        g_out = sem("g_out")

        block = ctx.enter_context(nc.Block())

        x_rows = x.rearrange("(j p) f -> p j f", p=P)
        out_rows = out.rearrange("(j p) f -> p j f", p=P)
        adj_stripes = adj.rearrange("(i p) n -> p i n", p=P)

        def apart(eng):
            eng.nop(nofuse=True)

        g_x = raw[0][:, 0:NB * D].rearrange("p (j f) -> p j f", f=D)
        g_x1 = raw[1][:, 0:NB * D].rearrange("p (j f) -> p j f", f=D)
        g_z = raw[2][:, 0:NB * D].rearrange("p (j f) -> p j f", f=D)
        g_chunk = raw[3][:, 0:GCH]
        g_chunkT = raw[3][:, GCH:2 * GCH]
        g_acc = agg[:, 0, :]
        g_rowsum = deg_inv[:, 1:2]

        @block.sync
        def _(sp):
            def load_half(t, c):
                stripe, half = 2 * t + c // 2, c % 2
                sp.dma_start(raw[c][:, :], adj_stripes[:, ds(stripe, 1), half * HALF:(half + 1) * HALF]
                             .rearrange("p a n -> p (a n)")).then_inc(raw_in[c], 16)

            sp.dma_start(packw_f, packw_in).then_inc(const_in, 16)
            sp.dma_start(ident[:, :], ident_in).then_inc(const_in, 16)
            sp.dma_start(w0_sb, w0).then_inc(const_in, 16)
            sp.dma_start(w1_sb[:, :], w1).then_inc(const_in, 16)
            load_half(0, 0)
            load_half(0, 1)
            sp.dma_start(resid[:, :, :], x_rows).then_inc(x_in, 16)
            load_half(0, 2)
            load_half(0, 3)
            with sp.Fori(1, NPAIR) as t:
                for c in range(SLOTS):
                    sp.wait_ge(half_packed, SLOTS * t + (c + 1 - SLOTS))
                    sp.wait_ge(half_checked, SLOTS * t + (c + 1 - SLOTS))
                    sp.wait_ge(half_checked_act, SLOTS * t + (c + 1 - SLOTS))
                    load_half(t, c)

            def store_pair(v):
                sp.dma_start(out_rows[:, ds(2 * v, 2), :], resid[:, ds(2 * v, 2), :]).then_inc(out_written, 16)

            with sp.Fori(0, NPAIR) as v:
                sp.wait_ge(normed, v + (NPAIR + 1))
                store_pair(v)
            sp.wait_ge(out_written, 16 * NPAIR)

            sp.wait_ge(flag_ready, 1)
            taken = sp.value_load(flag[0:1, 0:1], min_val=0, max_val=1)
            with sp.If(taken != 0):
                sp.dma_start(g_x, x_rows).then_inc(g_x_in, 16)
                sp.sem_inc(g_out, 16)
                for layer in range(2):
                    with sp.Fori(0, NB) as i:
                        with sp.Fori(0, GN) as c:
                            n = i * GN + c + layer * NB * GN
                            sp.wait_ge(g_chunk_free, n + 1)
                            sp.wait_ge(g_row_summed, n + 1)
                            sp.dma_start(g_chunk, adj_stripes[:, ds(i, 1), ds(c * GCH, GCH)]
                                         .rearrange("p a n -> p (a n)")).then_inc(g_chunk_in, 16)
                        if layer == 1:
                            sp.wait_ge(g_rows_ready, i + 2)
                            sp.dma_start(out_rows[:, ds(i, 1), :].rearrange("p a f -> p (a f)"), x1[:, 0, :])\
                              .then_inc(g_out, 16)
                sp.wait_ge(g_out, 16 * NB + 16)

        @block.tensor
        def _(pe):
            raw_hi = [r[:, :].bitcast(bf16) for r in raw]
            blocks = [spread[:, s, :, :, :].rearrange("p j s c -> p (j s c)").bitcast(fp8) for s in range(2)]

            def pack(t, s):
                if not isinstance(t, int) or t > 0:
                    pe.wait_ge(words_copied, 2 * t + (s - 1))
                for half in range(2):
                    c = 2 * s + half
                    pe.wait_ge(raw_in[c], 16 * t + 16)
                    for b in range(HB):
                        j = half * HB + b
                        n = PACKN if j * WPB + PACKN <= NB * WPB else WPB
                        last = nc.tensor.matmul(ps_words[s][:, j * WPB:j * WPB + n],
                                                raw_hi[c][:, 2 * P * b + 1:2 * P * (b + 1):2], packw[:, 0:n],
                                                start=True, stop=True)
                    last.then_inc(half_packed, 1)

            def product(t, s, known):
                pe.wait_ge(spread_done, 2 * t + (s + 1))
                if not isinstance(t, int) or t > 0:
                    pe.wait_ge(agg_read, 2 * t + (s - 1))
                apart(pe)
                for j in range(NB):
                    w = XW + ZW if j < known else XW
                    last = nc.tensor.matmul(ps_agg[:, s, 0:w], blocks[s][:, j * P:(j + 1) * P], xz[:, j, 0:w],
                                            start=(j == 0), stop=(j == NB - 1))
                last.then_inc(product_done, 1)

            late_blocks = [late[:, s, :, :, :].rearrange("p j s c -> p (j s c)").bitcast(fp8) for s in range(2)]

            def catch_up(n, g):
                pe.wait_ge(late_spread, n + 1)
                apart(pe)
                for s in range(2):
                    for j in range(KNOWN[g - 1], KNOWN[g]):
                        b = j - KNOWN[g - 1]
                        last = nc.tensor.matmul(ps_late[:, s, 0:ZW], late_blocks[s][:, b * P:(b + 1) * P],
                                                xz[:, j, XW:XW + ZW], start=(b == 0), stop=(j == KNOWN[g] - 1))
                last.then_inc(late_product, 1)

            def last_sums(v, r, s, lo, hi):
                bank = (ps_agg, ps_late)[r]
                for j in range(lo, hi):
                    b = s * (NB // 2) + j - LAST
                    last = nc.tensor.matmul(bank[:, s, 0:ZW], blocks[r][:, b * P:(b + 1) * P],
                                            xz[:, j, XW:XW + ZW], start=(j == LAST), stop=(j == NB - 1))
                if hi == NB and s == 1:
                    last.then_inc(last_product, 1)

            def transpose_cat(w):
                pe.wait_ge(cat_written, w + 1)
                for s in range(2):
                    last = nc.tensor.transpose(ps_transposed[:, s * P:(s + 1) * P], cat[:, s, :], ident[:, :])
                last.then_inc(cat_transposed, 1)

            def linear0(w):
                pe.wait_ge(catT_copied, w + 1)
                if not isinstance(w, int) or w > 0:
                    pe.wait_ge(z_rest_made, w)
                for s in range(2):
                    last = nc.tensor.matmul(ps_linear[:, s * D:(s + 1) * D], catT[:, s * P:(s + 1) * P], w0T[:, :],
                                            start=True, stop=True)
                last.then_inc(lin0_done, 1)

            def transpose_x1(w):
                pe.wait_ge(normed, w + 1)
                apart(pe)
                for s in range(2):
                    last = nc.tensor.transpose(ps_transposed[0:D, s * P:(s + 1) * P], x1[:, s, :], ident[:, :])
                last.then_inc(x1_transposed, 1)

            def linear1(w):
                pe.wait_ge(x1T_copied, w + 1)
                for s in range(2):
                    last = nc.tensor.matmul(ps_linear[:, s * D:(s + 1) * D], x1T[:, s * P:(s + 1) * P], w1_sb[:, :],
                                            start=True, stop=True)
                last.then_inc(z_done, 1)

            def pair_body(v, g, more=True):
                n = g * v + (LATE_BEFORE[g] - g * PPG * g)
                transpose_x1(v - 2)
                pack(v, 1)
                linear1(v - 2)
                if g > 2:
                    catch_up(n, g)
                product(v, 0, KNOWN[g])
                if g > 1:
                    catch_up(n + (g - 2), g)
                transpose_cat(v - 1)
                if more:
                    pack(v + 1, 0)
                linear0(v - 1)
                product(v, 1, KNOWN[g])
                if g > 0:
                    catch_up(n + (g - 1), g)

            pe.wait_ge(consts_made, 3)
            pack(0, 0)
            pack(0, 1)
            pe.wait_ge(const_in, 16 * 4)
            nc.tensor.transpose(ps_transposed[:, 0:D], w0_sb, ident[0:D, 0:D]).then_inc(w0_transposed, 1)
            pe.wait_ge(w0T_copied, 1)
            pe.wait_ge(x_split, 2)
            product(0, 0, 0)
            pack(1, 0)
            product(0, 1, 0)
            pack(1, 1)
            product(1, 0, 0)
            transpose_cat(0)
            pack(2, 0)
            linear0(0)
            product(1, 1, 0)
            for g in range(GROUPS):
                if g > 0:
                    pe.wait_ge(z_stored, KNOWN[g] // 2)
                with pe.Fori(max(2, g * PPG), min((g + 1) * PPG, NPAIR - 1)) as v:
                    pair_body(v, g)
            v = NPAIR - 1
            pair_body(v, GROUPS - 1, more=False)

            transpose_x1(v - 1)
            linear1(v - 1)
            pe.wait_ge(last_spread, 1)
            pe.wait_ge(agg_read, NB)
            last_sums(0, 0, 0, LAST, NB - LAG)
            transpose_cat(v)
            linear0(v)
            last_sums(0, 0, 1, LAST, NB - LAG)
            transpose_x1(v)
            linear1(v)
            pe.wait_ge(z_stored, NPAIR)
            for s in range(2):
                last_sums(0, 0, s, NB - LAG, NB)
            pe.wait_ge(last_spread, 2)
            pe.wait_ge(late_read, LATE_BEFORE[GROUPS])
            for s in range(2):
                last_sums(1, 1, s, LAST, NB)
            pe.wait_ge(bad_counted, 1)
            nc.tensor.matmul(ps_linear[0:1, 0:1], bad_row[:, :], ones[:, :], start=True, stop=True)\
              .then_inc(bad_summed, 1)
            with pe.Fori(1, NPAIR // 2) as q:
                for r in range(2):
                    v = 2 * q + r
                    pe.wait_ge(last_spread, v + 1)
                    pe.wait_ge(last_read, v - 1)
                    apart(pe)
                    for s in range(2):
                        last_sums(v, r, s, LAST, NB)

            pe.wait_ge(flag_ready, 1)
            taken = pe.value_load(flag[0:1, 0:1], min_val=0, max_val=1)
            with pe.If(taken != 0):
                pe.wait_ge(out_written, 16 * NPAIR)
                pe.wait_ge(g_x_in, 16)
                pe.sem_inc(g_chunk_free, 1)
                for layer, source in enumerate((g_x, g_z)):
                    with pe.Fori(0, NB) as i:
                        with pe.Fori(0, GN) as c:
                            n = i * GN + c + layer * NB * GN
                            pe.wait_ge(g_chunk_in, 16 * n + 16)
                            pe.wait_ge(g_added, n + 1)
                            for q in range(GQ):
                                last = nc.tensor.transpose(ps_words[0][:, q * P:(q + 1) * P],
                                                           g_chunk[:, q * P:(q + 1) * P], ident[:, :])
                            last.then_inc(g_chunk_free, 1)
                            pe.wait_ge(g_copied, n + 1)
                            for q in range(GQ):
                                last = nc.tensor.matmul(ps_agg[:, 0, 0:D], g_chunkT[:, q * P:(q + 1) * P],
                                                        source[:, ds(c * GQ + q, 1), :].rearrange("p a f -> p (a f)"),
                                                        start=(q == 0), stop=(q == GQ - 1))
                            last.then_inc(g_partial, 1)
                        if layer == 0:
                            pe.wait_ge(g_dve, 3 * i + 2)
                            nc.tensor.transpose(ps_transposed[:, 0:P], cat[:, 0, :], ident[:, :]).then_inc(g_pe, 1)
                            pe.wait_ge(g_act, 4 * i + 1)
                            nc.tensor.matmul(ps_linear[:, 0:D], catT[:, 0:P], w0T[:, :], start=True, stop=True)\
                              .then_inc(g_pe, 1)
                            pe.wait_ge(g_dve, 3 * i + 4)
                            apart(pe)
                            nc.tensor.transpose(ps_transposed[0:D, 0:P], x1[:, 0, :], ident[:, :]).then_inc(g_pe, 1)
                            pe.wait_ge(g_act, 4 * i + 3)
                            nc.tensor.matmul(ps_linear[:, 0:D], x1T[:, 0:P], w1_sb[:, :], start=True, stop=True)\
                              .then_inc(g_pe, 1)
                    if layer == 0:
                        pe.wait_ge(g_rows_ready, 1)

        @block.scalar
        def _(act):
            def copy_words(t, s, g):
                stripe_in_group = 2 * t + (s - SPG * g)
                act.wait_ge(half_packed, 4 * t + (2 * s + 2))
                if not isinstance(t, int) or 2 * t + s > 0:
                    act.wait_ge(spread_done, 2 * t + s)
                nc.scalar.activation(words_now[:, :], ps_words[s][:, :], ACT.Copy)
                nc.scalar.activation(words[g][:, ds(stripe_in_group, 1), :].rearrange("p a b -> p (a b)"),
                                     ps_words[s][:, KNOWN[g] * WPB:NB * WPB], ACT.Copy).then_inc(words_copied, 1)

            def copy_catT(w):
                act.wait_ge(cat_transposed, w + 1)
                nc.scalar.activation(catT[:, :], ps_transposed[:, 0:2 * P], ACT.Copy).then_inc(catT_copied, 1)

            def copy_x1T(w):
                act.wait_ge(x1_transposed, w + 1)
                nc.scalar.activation(x1T[:, :], ps_transposed[0:D, 0:2 * P], ACT.Copy).then_inc(x1T_copied, 1)

            def standard_deviation(n, r, eps):
                act.wait_ge(var_ready, n + 1)
                nc.scalar.activation(std[:, r, :], meanvar[:, r, :, 1], ACT.Sqrt, bias=eps[:, :]).then_inc(std_ready, 1)

            def store_z_hi(w):
                act.wait_ge(z_done, w + 1)
                nc.scalar.activation(xz[:, ds(2 * w, 2), XW:XW + D], ps_linear_v, ACT.Copy).then_inc(z_hi_stored, 1)

            upper = [r[:, 0:ACOLS].bitcast(u16)[:, 1::2] for r in raw]
            lower = [r[:, 0:ACOLS].bitcast(u16)[:, 0::2] for r in raw]

            def check(t, c):
                act.wait_ge(raw_in[c], 16 * t + 16)
                if not isinstance(t, int) or 4 * t + c > 0:
                    act.wait_ge(half_checked_act, 4 * t + c)
                apart(act)
                nc.scalar.activation(verdict[:, ACOLS:2 * ACOLS], upper[c], ACT.Relu, bias=minus_one_hi[:, :], scale=1.0 / DOWN,
                                     accum_out=above_one[:, ds(4 * t + c, 1)])
                nc.scalar.activation(verdict[:, 2 * ACOLS:3 * ACOLS], upper[c], ACT.Abs, bias=minus_middle[:, :], scale=1.0 / DOWN,
                                     accum_out=from_middle[:, ds(4 * t + c, 1)])
                nc.scalar.activation(verdict[:, 0:ACOLS], lower[c], ACT.Copy, scale=1.0 / DOWN,
                                     accum_out=low_bits[:, ds(4 * t + c, 1)]).then_inc(half_checked_act, 1)

            def pair_body(u, g):
                copy_catT(u - 2)
                check(u, 0)
                copy_words(u, 0, g)
                check(u, 1)
                standard_deviation(u - 2, 0, eps1)
                copy_x1T(u - 2)
                check(u, 2)
                copy_words(u, 1, g)
                store_z_hi(u - 2)
                check(u, 3)

            act.wait_ge(consts_made, 3)
            check(0, 0)
            check(0, 1)
            copy_words(0, 0, 0)
            act.wait_ge(x_in, 16)
            for q in range(2):
                nc.scalar.activation(xz[:, q * QX:(q + 1) * QX, 0:D], resid[:, q * QX:(q + 1) * QX, :], ACT.Copy)\
                  .then_inc(x_hi_stored, 1)
            for q in range(2):
                act.wait_ge(x_rest_made, q + 1)
                nc.scalar.activation(xz[:, q * QX:(q + 1) * QX, D:2 * D], x_rest[q], ACT.Copy)\
                  .then_inc(x_mid_stored, 1)
            check(0, 2)
            check(0, 3)
            copy_words(0, 1, 0)
            act.wait_ge(w0_transposed, 1)
            nc.scalar.activation(w0T[:, :], ps_transposed[:, 0:D], ACT.Copy).then_inc(w0T_copied, 1)
            check(1, 0)
            check(1, 1)
            copy_words(1, 0, 0)
            check(1, 2)
            check(1, 3)
            copy_words(1, 1, 0)
            for g in range(GROUPS):
                with act.Fori(max(2, g * PPG), (g + 1) * PPG) as u:
                    pair_body(u, g)
            w = NPAIR - 2
            copy_catT(w)
            standard_deviation(w, 0, eps1)
            copy_x1T(w)
            store_z_hi(w)
            copy_catT(w + 1)
            standard_deviation(w + 1, 0, eps1)
            copy_x1T(w + 1)
            store_z_hi(w + 1)
            with act.Fori(0, NPAIR // 2) as q:
                for r in range(2):
                    standard_deviation(2 * q + (r + NPAIR), r, eps4)

            act.wait_ge(flag_ready, 1)
            taken = act.value_load(flag[0:1, 0:1], min_val=0, max_val=1)
            with act.If(taken != 0):
                act.wait_ge(out_written, 16 * NPAIR)
                for layer in range(2):
                    with act.Fori(0, NB) as i:
                        with act.Fori(0, GN) as c:
                            n = i * GN + c + layer * NB * GN
                            act.wait_ge(g_chunk_free, n + 2)
                            nc.scalar.activation(g_chunkT, ps_words[0][:, :], ACT.Copy).then_inc(g_copied, 1)
                        if layer == 0:
                            act.wait_ge(g_pe, 4 * i + 1)
                            nc.scalar.activation(catT[:, 0:P], ps_transposed[:, 0:P], ACT.Copy).then_inc(g_act, 1)
                            act.wait_ge(g_dve, 3 * i + 3)
                            nc.scalar.activation(std[:, 0, 0:1], meanvar[:, 0, 0, 1:2], ACT.Sqrt, bias=eps1[:, :])\
                              .then_inc(g_act, 1)
                            act.wait_ge(g_pe, 4 * i + 3)
                            nc.scalar.activation(x1T[:, 0:P], ps_transposed[0:D, 0:P], ACT.Copy).then_inc(g_act, 1)
                            act.wait_ge(g_pe, 4 * i + 4)
                            nc.scalar.activation(g_z[:, ds(i, 1), :].rearrange("p a f -> p (a f)"), ps_linear[:, 0:D],
                                                 ACT.Copy).then_inc(g_act, 1)
                        else:
                            act.wait_ge(g_dve, i + (3 * NB + 2))
                            nc.scalar.activation(std[:, 0, 0:1], meanvar[:, 0, 0, 1:2], ACT.Sqrt, bias=eps1[:, :])\
                              .then_inc(g_act, 1)

        @block.vector
        def _(dve):
            now_lanes = words_now[:, :].bitcast(u32).rearrange("p (j c) -> p j c", c=UPB)

            def check(t, s, half):
                c = 2 * s + half
                dve.wait_ge(raw_in[c], 16 * t + 16)
                if not isinstance(t, int) or 4 * t + c > 0:
                    dve.wait_ge(half_checked, 4 * t + c)
                nc.vector.scalar_tensor_tensor(verdict[:, 3 * ACOLS:], raw[c][:, ACOLS:], 0.0, raw[c][:, ACOLS:], ALU.is_gt, ALU.not_equal,
                                               accum_out=bad[:, ds(4 * t + c, 1)]).then_inc(half_checked, 1)

            def spread_bits(out, lanes):
                for k in range(SHIFTS):
                    op = ALU.logical_shift_left if k <= TWO_FP8 else ALU.logical_shift_right
                    last = nc.vector.tensor_scalar(out(k), lanes, abs(TWO_FP8 - k), TWO_MASK, op, ALU.bitwise_and)
                return last

            def spread_now(t, s):
                dve.wait_ge(words_copied, 2 * t + (s + 1))
                if not isinstance(t, int) or t > 0:
                    dve.wait_ge(product_done, 2 * t + (s - 1))
                spread_bits(lambda k: spread[:, s, :, k, :], now_lanes).then_inc(spread_done, 1)

            def kept_lanes(g, pair, lo, hi):
                return words[g][:, ds(2 * pair, 2), (lo - KNOWN[g]) * WPB:(hi - KNOWN[g]) * WPB].bitcast(u32)\
                    .rearrange("p a (j c) -> p a j c", c=UPB)

            def read_late(n):
                dve.wait_ge(late_product, n + 1)
                if not isinstance(n, int) or n > 0:
                    dve.wait_ge(late_added, n)
                for s in range(2):
                    last = nc.vector.tensor_reduce(late_sum[:, s, :],
                                                   ps_late[:, s, 0:ZW].rearrange("p (k f) -> p f k", k=3),
                                                   axis=AX, op=ALU.add)
                last.then_inc(late_read, 1)

            def spread_late(u, g, k, first=False):
                n = g * u + (LATE_BEFORE[g] - g * PPG * g + k)
                if not first:
                    read_late(n - 1)
                lanes = kept_lanes(k, u - PPG * g, KNOWN[g - 1], KNOWN[g])
                spread_bits(lambda b: late[:, :, 0:KNOWN[g] - KNOWN[g - 1], b, :], lanes).then_inc(late_spread, 1)

            def spread_last(v, r, g):
                lanes = kept_lanes(g, v - PPG * g, LAST, NB)
                out = spread[:, r, :, :, :].rearrange("p (a j) k c -> p a j k c", a=2)
                spread_bits(lambda k: out[:, :, 0:NB - LAST, k, :], lanes).then_inc(last_spread, 1)

            def read_sums(w, s, with_z):
                dve.wait_ge(product_done, 2 * w + (s + 1))
                if s == 0 and (not isinstance(w, int) or w > 0):
                    dve.wait_ge(cat_written, w)
                nc.vector.tensor_reduce(agg[:, s, :], ps_agg[:, s, 0:3 * D].rearrange("p (k f) -> p f k", k=3),
                                        axis=AX, op=ALU.add)
                if with_z:
                    nc.vector.tensor_reduce(part[:, s, :], ps_agg[:, s, XW:XW + ZW].rearrange("p (k f) -> p f k", k=3),
                                            axis=AX, op=ALU.add)
                nc.vector.tensor_scalar(deg[:, s:s + 1], ps_agg[:, s, 3 * D:3 * D + 1], 2.0, None, ALU.max)\
                  .then_inc(agg_read, 1)

            def invert_degree(w):
                dve.wait_ge(agg_read, 2 * w + 2)
                nc.vector.reciprocal(deg_inv[:, :], deg[:, :]).then_inc(deg_inverted, 1)

            def moments(n, r):
                dve.wait_ge(h_written, n + 1)
                for s in range(2):
                    last = nc.vector.bn_stats(stats[:, s, :], h[r][:, s, :])
                last.then_inc(stats_written, 1)
                dve.wait_ge(stats_written, n + 1)
                apart(dve)
                for s in range(2):
                    last = nc.vector.bn_aggr(meanvar[:, r, s, :], stats[:, s, :])
                last.then_inc(var_ready, 1)

            def residual1(w):
                dve.wait_ge(lin0_done, w + 1)
                nc.vector.scalar_tensor_tensor(h[0][:, :, :], ps_linear_v, 0.0, resid[:, ds(2 * w, 2), :], ALU.max, ALU.add)\
                  .then_inc(h_written, 1)
                moments(w, 0)

            def invert_std(n, r=0):
                dve.wait_ge(std_ready, n + 1)
                nc.vector.reciprocal(rstd[:, r, :], std[:, r, :]).then_inc(rstd_ready, 1)

            def z_minus_hi(w):
                dve.wait_ge(z_hi_stored, w + 1)
                nc.vector.tensor_tensor(z_rest[:, :, :], ps_linear_v, xz[:, ds(2 * w, 2), XW:XW + D], ALU.subtract)\
                  .then_inc(z_rest_made, 1)

            def pair_body(u, g, first=False):
                with_z = g > 0 and not first
                for half in range(2):
                    check(u, 0, half)
                residual1(u - 2)
                spread_now(u, 0)
                invert_std(u - 2)
                read_sums(u - 1, 0, with_z)
                if g > 2:
                    spread_late(u, g, 0)
                check(u, 1, 0)
                if g > 1:
                    spread_late(u, g, g - 2)
                check(u, 1, 1)
                z_minus_hi(u - 2)
                spread_now(u, 1)
                read_sums(u - 1, 1, with_z)
                invert_degree(u - 1)
                if g > 0:
                    spread_late(u, g, g - 1, first)

            nc.vector.memset(minus_one_hi[:, :], -float(ONE_HI // DOWN))
            nc.vector.memset(minus_middle[:, :], -float(ONE_HI // DOWN // 2))
            nc.vector.memset(ones[:, :], 1.0)
            nc.vector.memset(eps1[:, :], EPS).then_inc(consts_made, 1)
            nc.vector.memset(eps4[:, :], 4 * EPS).then_inc(consts_made, 1)
            nc.vector.memset(xz[:, :, 3 * D:3 * D + 1], 1.0)
            dve.wait_ge(const_in, 16 * 4)
            nc.vector.tensor_copy(packw[:, :], packw_f).then_inc(consts_made, 1)
            for half in range(2):
                check(0, 0, half)
            spread_now(0, 0)
            for q in range(2):
                dve.wait_ge(x_hi_stored, q + 1)
                nc.vector.tensor_tensor(x_rest[q], resid[:, q * QX:(q + 1) * QX, :], xz[:, q * QX:(q + 1) * QX, 0:D],
                                        ALU.subtract).then_inc(x_rest_made, 1)
            for q in range(2):
                dve.wait_ge(x_mid_stored, q + 1)
                nc.vector.tensor_tensor(xz[:, q * QX:(q + 1) * QX, 2 * D:3 * D], x_rest[q],
                                        xz[:, q * QX:(q + 1) * QX, D:2 * D], ALU.subtract).then_inc(x_split, 1)
            for half in range(2):
                check(0, 1, half)
            spread_now(0, 1)
            for half in range(2):
                check(1, 0, half)
            spread_now(1, 0)
            read_sums(0, 0, False)
            for half in range(2):
                check(1, 1, half)
            spread_now(1, 1)
            read_sums(0, 1, False)
            invert_degree(0)
            with dve.Fori(2, PPG) as u:
                pair_body(u, 0)
            pair_body(PPG, 1, first=True)
            for g in range(1, GROUPS):
                with dve.Fori(max(PPG + 1, g * PPG), (g + 1) * PPG) as u:
                    pair_body(u, g)
            w = NPAIR - 2
            dve.wait_ge(half_checked, 4 * NPAIR)
            dve.wait_ge(half_checked_act, 4 * NPAIR)
            for n, (sums, right_sum) in enumerate(((from_middle, float(ACOLS * (ONE_HI // DOWN // 2))),
                                                   (above_one, 0.0), (low_bits, 0.0))):
                nc.vector.scalar_tensor_tensor(bad[:, :], sums[:, :], right_sum, bad[:, :], ALU.not_equal, ALU.add)\
                  .then_inc(bad_listed, 1)
                dve.wait_ge(bad_listed, n + 1)
            nc.vector.tensor_reduce(bad_row[:, :], bad[:, :], axis=AX, op=ALU.add).then_inc(bad_counted, 1)
            residual1(w)
            dve.wait_ge(product_done, NB - 1)
            spread_last(0, 0, 0)
            invert_std(w)
            read_sums(w + 1, 0, True)
            read_sums(w + 1, 1, True)
            invert_degree(w + 1)
            spread_last(1, 1, 0)
            read_late(LATE_BEFORE[GROUPS] - 1)
            z_minus_hi(w)
            residual1(w + 1)
            invert_std(w + 1)
            z_minus_hi(w + 1)

            def read_last(v, r):
                bank = (ps_agg, ps_late)[r]
                dve.wait_ge(last_product, v + 1)
                for s in range(2):
                    last = nc.vector.tensor_reduce(agg[:, s, :], bank[:, s, 0:ZW].rearrange("p (k f) -> p f k", k=3),
                                                   axis=AX, op=ALU.add)
                last.then_inc(last_read, 1)

            def residual2(v, r):
                dve.wait_ge(last_read, v + 1)
                dve.wait_ge(normed, v + (NPAIR - 1))
                nc.vector.tensor_tensor(h[r][:, :, :], agg[:, :, :], resid[:, ds(2 * v, 2), :], ALU.add)\
                  .then_inc(h_written, 1)
                moments(v + NPAIR, r)

            def pair_body2(v, r, g, first=False):
                dve.wait_ge(last_product, v - 1)
                spread_last(v, r, g)
                if not first:
                    invert_std(v - 3 + NPAIR, 1 - r)
                read_last(v - 2, r)
                residual2(v - 2, r)

            dve.wait_ge(resid_written, NPAIR)
            dve.wait_ge(late_added, LATE_BEFORE[GROUPS])
            pair_body2(2, 0, 0, first=True)
            pair_body2(3, 1, 0)
            for g in range(GROUPS):
                with dve.Fori(max(2, g * PPG // 2), (g + 1) * PPG // 2) as q:
                    for r in range(2):
                        pair_body2(2 * q + r, r, g)
            dve.wait_ge(bad_summed, 1)
            nc.vector.tensor_scalar(flag[:, :], ps_linear[0:1, 0:1], 0.0, None, ALU.is_gt).then_inc(flag_ready, 1)
            invert_std(2 * NPAIR - 3, 1)
            read_last(NPAIR - 2, 0)
            residual2(NPAIR - 2, 0)
            invert_std(2 * NPAIR - 2, 0)
            read_last(NPAIR - 1, 1)
            residual2(NPAIR - 1, 1)
            invert_std(2 * NPAIR - 1, 1)

            dve.wait_ge(flag_ready, 1)
            taken = dve.value_load(flag[0:1, 0:1], min_val=0, max_val=1)
            with dve.If(taken != 0):
                dve.wait_ge(out_written, 16 * NPAIR)
                dve.wait_ge(g_x_in, 16)
                dve.sem_inc(g_row_summed, 1)
                dve.sem_inc(g_added, 1)
                nc.vector.memset(deg_inv[:, :], 0.0).then_inc(g_dve, 1)

                def g_normalise(rows, m):
                    nc.vector.bn_stats(stats[:, 0, :], h[0][:, 0, :]).then_inc(stats_written, 1)
                    dve.drain()
                    nc.vector.bn_aggr(meanvar[:, 0, 0, :], stats[:, 0, :]).then_inc(g_dve, 1)
                    dve.wait_ge(g_act, m)
                    nc.vector.reciprocal(rstd[:, 0, 0:1], std[:, 0, 0:1])
                    dve.drain()
                    return nc.vector.tensor_scalar(rows, h[0][:, 0, :], meanvar[:, 0, 0, 0:1], rstd[:, 0, 0:1],
                                                   ALU.subtract, ALU.mult)

                for layer in range(2):
                    with dve.Fori(0, NB) as i:
                        nc.vector.memset(g_acc, 0.0)
                        nc.vector.memset(deg[:, 0:1], 0.0)
                        dve.drain()
                        with dve.Fori(0, GN) as c:
                            n = i * GN + c + layer * NB * GN
                            dve.wait_ge(g_chunk_in, 16 * n + 16)
                            nc.vector.tensor_reduce(g_rowsum, g_chunk, axis=AX, op=ALU.add).then_inc(g_row_summed, 1)
                            dve.drain()
                            nc.vector.tensor_tensor(deg[:, 0:1], deg[:, 0:1], g_rowsum, ALU.add)
                            dve.wait_ge(g_partial, n + 1)
                            nc.vector.tensor_tensor(g_acc, g_acc, ps_agg[:, 0, 0:D], ALU.add).then_inc(g_added, 1)
                            dve.drain()
                        if layer == 0:
                            nc.vector.tensor_scalar(deg[:, 1:2], deg[:, 0:1], 1.0, None, ALU.max)
                            dve.drain()
                            nc.vector.reciprocal(deg_inv[:, 0:1], deg[:, 1:2])
                            nc.vector.tensor_copy(cat[:, 0, 0:D], g_x[:, ds(i, 1), :].rearrange("p a f -> p (a f)"))
                            dve.drain()
                            nc.vector.tensor_scalar(cat[:, 0, D:2 * D], g_acc, deg_inv[:, 0:1], None, ALU.mult)\
                              .then_inc(g_dve, 1)
                            dve.wait_ge(g_pe, 4 * i + 2)
                            nc.vector.scalar_tensor_tensor(h[0][:, 0, :], ps_linear[:, 0:D], 0.0,
                                                           g_x[:, ds(i, 1), :].rearrange("p a f -> p (a f)"),
                                                           ALU.max, ALU.add)
                            dve.drain()
                            g_normalise(x1[:, 0, :], 4 * i + 2).then_inc(g_dve, 1)
                            dve.drain()
                            nc.vector.tensor_copy(g_x1[:, ds(i, 1), :].rearrange("p a f -> p (a f)"), x1[:, 0, :])
                            dve.wait_ge(g_act, 4 * i + 4)
                        else:
                            nc.vector.tensor_tensor(h[0][:, 0, :], g_acc,
                                                    g_x1[:, ds(i, 1), :].rearrange("p a f -> p (a f)"), ALU.add)
                            dve.drain()
                            g_normalise(x1_twice[:, 0, :], i + (4 * NB + 1))
                            dve.drain()
                            dve.wait_ge(g_out, 16 * i + 16)
                            nc.vector.tensor_copy(x1[:, 0, :], x1_twice[:, 0, :]).then_inc(g_rows_ready, 1)
                    if layer == 0:
                        nc.vector.memset(x1[:, 1, :], 0.0).then_inc(g_rows_ready, 1)

        @block.gpsimd
        def _(pool):
            def write_cat(w, with_z):
                pool.wait_ge(deg_inverted, w + 1)
                if not isinstance(w, int) or w > 0:
                    pool.wait_ge(cat_transposed, w)
                if with_z:
                    pool.wait_ge(resid_written, w)
                apart(pool)
                if with_z:
                    nc.gpsimd.tensor_copy(part_kept[:, :, :], part[:, :, :])
                nc.gpsimd.tensor_copy(cat[:, :, 0:D], resid[:, ds(2 * w, 2), :])
                nc.gpsimd.tensor_tensor(cat[:, :, D:2 * D], agg[:, :, :],
                                        deg_inv[:, :].unsqueeze(2).to_broadcast([P, 2, D]), ALU.mult)\
                  .then_inc(cat_written, 1)

            def normalise(n):
                pool.wait_ge(rstd_ready, n + 1)
                apart(pool)
                for s in range(2):
                    last = nc.gpsimd.tensor_scalar(x1[:, s, :], h[0][:, s, :], meanvar[:, 0, s, 0:1], rstd[:, 0, s:s + 1],
                                                   ALU.subtract, ALU.mult)
                last.then_inc(normed, 1)

            def keep_x1(w, with_z):
                normalise(w)
                pool.wait_ge(normed, w + 1)
                apart(pool)
                if with_z:
                    nc.gpsimd.tensor_tensor(x1_twice[:, :, :], x1[:, :, :], x1[:, :, :], ALU.add)\
                      .then_inc(x1_doubled, 1)
                    pool.wait_ge(x1_doubled, w - (PPG - 1))
                    apart(pool)
                    nc.gpsimd.tensor_tensor(resid[:, ds(2 * w, 2), :], x1_twice[:, :, :], part_kept[:, :, :], ALU.add)\
                      .then_inc(resid_written, 1)
                else:
                    nc.gpsimd.tensor_tensor(resid[:, ds(2 * w, 2), :], x1[:, :, :], x1[:, :, :], ALU.add)\
                      .then_inc(resid_written, 1)

            def store_z(w):
                pool.wait_ge(z_rest_made, w + 1)
                apart(pool)
                nc.gpsimd.tensor_copy(xz[:, ds(2 * w, 2), XW + D:XW + 2 * D], z_rest[:, :, :])\
                  .then_inc(z_mid_stored, 1)
                pool.wait_ge(z_mid_stored, w + 1)
                apart(pool)
                nc.gpsimd.tensor_tensor(xz[:, ds(2 * w, 2), XW + 2 * D:XW + 3 * D], z_rest[:, :, :],
                                        xz[:, ds(2 * w, 2), XW + D:XW + 2 * D], ALU.subtract).then_inc(z_stored, 1)

            def add_late(n, pair):
                pool.wait_ge(late_read, n + 1)
                apart(pool)
                rows = resid[:, ds(2 * pair, 2), :]
                nc.gpsimd.tensor_tensor(rows, rows, late_sum[:, :, :], ALU.add).then_inc(late_added, 1)

            def add_last_of(g, u):
                add_late(g * u + (LATE_BEFORE[g] - g * PPG * g + g - 1), u - PPG * g + (g - 1) * PPG)

            def pair_body(u, g, first=False):
                with_z = g > 1 or (g == 1 and not first)
                n = g * u + (LATE_BEFORE[g] - g * PPG * g)
                keep_x1(u - 2, (g > 0 and not isinstance(u, int)) or (isinstance(u, int) and u - 2 >= PPG))
                if g > 2:
                    add_last_of(*((g - 1, u - 1) if first else (g, u - 1)))
                    add_late(n, u - PPG * g)
                if g == 2:
                    add_last_of(*((g - 1, u - 1) if first else (g, u - 1)))
                store_z(u - 2)
                write_cat(u - 1, with_z)
                if g == 1 and not first:
                    add_last_of(g, u - 1)
                if g > 1:
                    add_late(n + g - 2, u - PPG * g + (g - 2) * PPG)

            write_cat(0, False)
            with pool.Fori(2, PPG) as u:
                pair_body(u, 0)
            pair_body(PPG, 1, first=True)
            pair_body(PPG + 1, 1)
            with pool.Fori(PPG + 2, 2 * PPG) as u:
                pair_body(u, 1)
            for g in range(2, GROUPS):
                pair_body(g * PPG, g, first=True)
                with pool.Fori(g * PPG + 1, (g + 1) * PPG) as u:
                    pair_body(u, g)
            keep_x1(NPAIR - 2, True)
            write_cat(NPAIR - 1, True)
            add_last_of(GROUPS - 1, NPAIR - 1)
            store_z(NPAIR - 2)
            keep_x1(NPAIR - 1, True)
            store_z(NPAIR - 1)

            def normalise_last(v, r):
                pool.wait_ge(rstd_ready, v + (NPAIR + 1))
                pool.wait_ge(normed, v + NPAIR)
                apart(pool)
                nc.gpsimd.tensor_tensor(x1[:, :, :], h[r][:, :, :], meanvar[:, r, :, 0:1].to_broadcast([P, 2, D]),
                                        ALU.subtract).then_inc(centred, 1)
                pool.wait_ge(centred, v + 1)
                apart(pool)
                nc.gpsimd.tensor_tensor(resid[:, ds(2 * v, 2), :], x1[:, :, :],
                                        rstd[:, r, :].unsqueeze(2).to_broadcast([P, 2, D]), ALU.mult)\
                  .then_inc(normed, 1)

            pool.wait_ge(x1_transposed, NPAIR)
            with pool.Fori(0, NPAIR // 2) as q:
                for r in range(2):
                    normalise_last(2 * q + r, r)


_INS = ['x', 'adj', 'L0_gnn_W', 'L1_gnn_weight']


def kernel(**inputs):
    import numpy as _np
    import concourse.bacc as _bacc
    from concourse import mybir as _mybir
    from concourse.bass_utils import run_bass_kernel_spmd as _run

    nc = _bacc.Bacc("TRN2", target_bir_lowering=False, num_devices=1)
    arrays, args = {}, []
    named = [(name, _np.ascontiguousarray(inputs[name])) for name in _INS]
    named += [("pack_weights", pack_weights()), ("identity", _np.eye(P, dtype=_np.float32))]
    for name, a in named:
        arrays[f"in_{name}_dram"] = a
        args.append(nc.dram_tensor(f"in_{name}_dram", a.shape, _mybir.dt.from_np(a.dtype), kind="ExternalInput").ap())
    args.append(nc.dram_tensor("out_0_dram", (N, D), _mybir.dt.float32, kind="ExternalOutput").ap())
    gnn_kernel(nc, *args)
    r = _run(nc, [arrays], core_ids=[0])
    return r.results[0]["out_0_dram"]
```

```python
from contextlib import ExitStack

import numpy as np
import concourse.bass as bass
from concourse import mybir

P = 128
N = 8192
D = 64
NB = N // P
NPAIR = NB // 2
EPS = 1e-5

HALF = N // 2
HB = NB // 2
SLOTS = 4

ACOLS = 1024
ONE_HI = 0x3F80
DOWN = 64

BITS = 16
WPB = P // BITS
PACKN = 64
UPB = WPB // 2
SHIFTS = 8
TWO_FP8 = 6
TWO_MASK = 0x40404040

GROUPS = 4
PPG = NPAIR // GROUPS
SPG = NB // GROUPS
LAG = 4
KNOWN = [max(0, SPG * g - LAG) for g in range(GROUPS)]
HALVES = 2 * GROUPS
PPH = NPAIR // HALVES
KNOWN_HALF = [max(0, SPG // 2 * e - LAG) for e in range(HALVES)]

CAUGHT_IN = ((), (), (0, 1), (0, 1, 2), (0, 2), (1, 3), (0, 2, 4), (1, 3, 5))
CAUGHT_TO = KNOWN_HALF[:4] + [KNOWN[2]] * 2 + [KNOWN[3]] * 2


def catch_ups():
    done, items = list(KNOWN_HALF), []
    for e in range(HALVES):
        items.append([(k, done[k], CAUGHT_TO[e]) for k in CAUGHT_IN[e]])
        for k in CAUGHT_IN[e]:
            done[k] = CAUGHT_TO[e]
    assert done == [KNOWN[GROUPS - 1]] * (HALVES - 1) + [KNOWN_HALF[HALVES - 1]]
    return items


CATCH = catch_ups()
LATE = max(hi - lo for items in CATCH for _, lo, hi in items)
LATE_BEFORE = [PPH * sum(len(items) for items in CATCH[:e]) for e in range(HALVES + 1)]
LAST = KNOWN[GROUPS - 1]
LAST_HALF = KNOWN_HALF[HALVES - 1]


def late_count(e, u, i):
    return len(CATCH[e]) * u + (LATE_BEFORE[e] - len(CATCH[e]) * PPH * e + i)


def late_pair(e, u, i):
    return u + PPH * (CATCH[e][i][0] - e)


XW = 3 * D + 1
ZW = 3 * D
XZ = XW + ZW + 1

GCH = 512
GQ = GCH // P
GN = N // GCH


def pack_weights():
    w = np.zeros((P, PACKN), np.float32)
    for i in range(P):
        w[i, (i % BITS) // 2] = 2.0 ** (8 * (i % 2) + i // BITS)
    return w


def gnn_kernel(nc, x, adj, w0, w1, packw_in, ident_in, out):
    fp32, bf16, u8 = mybir.dt.float32, mybir.dt.bfloat16, mybir.dt.uint8
    u16, u32, i32, fp8 = mybir.dt.uint16, mybir.dt.uint32, mybir.dt.int32, mybir.dt.float8e4
    ALU = mybir.AluOpType
    ACT = mybir.ActivationFunctionType
    AX = mybir.AxisListType.X
    ds = bass.ds

    ctx = ExitStack()
    with ctx:
        def sb(name, shape, dt):
            return ctx.enter_context(nc.sbuf_tensor(name, shape, dt))

        def pb(name, shape, dt):
            return ctx.enter_context(nc.psum_tensor(name, shape, dt))

        def sem(name):
            return ctx.enter_context(nc.semaphore(name))

        raw = [sb(f"raw{c}", [P, HALF], fp32) for c in range(SLOTS)]
        words = [sb(f"words{g}", [P, SPG, (NB - KNOWN[g]) * WPB], u16) for g in range(GROUPS)]
        words_now = sb("words_now", [P, NB * WPB], u16)
        spread = sb("spread", [P, 2, NB, SHIFTS, UPB], u32)
        xz = sb("xz", [P, NB, XZ], bf16)
        resid = sb("resid", [P, NB, D], fp32)
        verdict = sb("verdict", [P, HALF - ACOLS + 3 * ACOLS], u8)
        above_one = sb("above_one", [P, 2 * NB], fp32)
        from_middle = sb("from_middle", [P, 2 * NB], fp32)
        low_bits = sb("low_bits", [P, 2 * NB], fp32)
        minus_one_hi = sb("minus_one_hi", [P, 1], fp32)
        minus_middle = sb("minus_middle", [P, 1], fp32)
        bad = sb("bad", [P, 2 * NB], fp32)
        bad_row = sb("bad_row", [P, 1], fp32)
        flag = sb("flag", [1, 1], i32)
        ident = sb("ident", [P, P], fp32)
        packw = sb("packw", [P, PACKN], bf16)
        ones = sb("ones", [P, 1], fp32)
        eps1 = sb("eps1", [P, 1], fp32)
        eps4 = sb("eps4", [P, 1], fp32)
        w0T = sb("w0T", [2 * D, D], fp32)
        w1_sb = sb("w1_sb", [D, D], fp32)
        agg = sb("agg", [P, 2, D], fp32)
        part = sb("part", [P, 2, D], fp32)
        late = sb("late", [P, 2, LATE, SHIFTS, UPB], u32)
        late_sum = sb("late_sum", [P, 2, D], fp32)
        part_kept = sb("part_kept", [P, 2, D], fp32)
        deg = sb("deg", [P, 2], fp32)
        deg_inv = sb("deg_inv", [P, 2], fp32)
        cat = sb("cat", [P, 2, 2 * D], fp32)
        w0_sb = cat[0:D, 0, :]
        catT = sb("catT", [2 * D, 2 * P], fp32)
        stats = sb("stats", [P, 2, 6], fp32)
        meanvar = sb("meanvar", [P, 2, 2, 2], fp32)
        std = sb("std", [P, 2, 2], fp32)
        rstd = sb("rstd", [P, 2, 2], fp32)
        x1 = sb("x1", [P, 2, D], fp32)
        x1_twice = sb("x1_twice", [P, 2, D], fp32)
        hidden = [sb("h0", [P, 2, D], fp32), x1_twice]
        x1T = catT[0:D, :]
        z_rest = sb("z_rest", [P, 2, D], fp32)
        packw_f = z_rest[:, :, :].rearrange("p a f -> p (a f)")[:, 0:PACKN]

        ps_words = [pb(f"ps_words{i}", [P, 512], fp32) for i in range(2)]
        ps_agg = pb("ps_agg", [P, 2, 512], fp32)
        ps_late = pb("ps_late", [P, 2, 512], fp32)
        ps_transposed = pb("ps_transposed", [P, 512], fp32)
        ps_linear = pb("ps_linear", [P, 512], fp32)
        ps_linear_v = ps_linear[:, 0:2 * D].rearrange("p (a f) -> p a f", a=2)

        QX = NB // 2
        x_rest = [words[1 + q][:, :, :].rearrange("p a b -> p (a b)")[:, 0:QX * D * 2].bitcast(fp32)
                  .rearrange("p (j f) -> p j f", f=D) for q in range(2)]

        raw_in = [sem(f"raw_in{c}") for c in range(SLOTS)]
        x_in = sem("x_in")
        const_in = sem("const_in")
        out_written = sem("out_written")
        consts_made = sem("consts_made")
        w0_transposed = sem("w0_transposed")
        w0T_copied = sem("w0T_copied")
        x_hi_stored = sem("x_hi_stored")
        x_rest_made = sem("x_rest_made")
        x_mid_stored = sem("x_mid_stored")
        x_split = sem("x_split")
        half_packed = sem("half_packed")
        half_checked = sem("half_checked")
        half_checked_act = sem("half_checked_act")
        bad_listed = sem("bad_listed")
        words_copied = sem("words_copied")
        spread_done = sem("spread_done")
        product_done = sem("product_done")
        agg_read = sem("agg_read")
        late_spread = sem("late_spread")
        late_product = sem("late_product")
        late_read = sem("late_read")
        late_added = sem("late_added")
        last_spread = sem("last_spread")
        last_product = sem("last_product")
        last_read = sem("last_read")
        centred = sem("centred")
        deg_inverted = sem("deg_inverted")
        cat_written = sem("cat_written")
        cat_transposed = sem("cat_transposed")
        catT_copied = sem("catT_copied")
        lin0_done = sem("lin0_done")
        h_written = sem("h_written")
        stats_written = sem("stats_written")
        var_ready = sem("var_ready")
        std_ready = sem("std_ready")
        rstd_ready = sem("rstd_ready")
        normed = sem("normed")
        x1_doubled = sem("x1_doubled")
        resid_written = sem("resid_written")
        x1_transposed = sem("x1_transposed")
        x1T_copied = sem("x1T_copied")
        z_done = sem("z_done")
        z_hi_stored = sem("z_hi_stored")
        z_rest_made = sem("z_rest_made")
        z_mid_stored = sem("z_mid_stored")
        z_stored = sem("z_stored")
        bad_counted = sem("bad_counted")
        bad_summed = sem("bad_summed")
        flag_ready = sem("flag_ready")
        g_x_in = sem("g_x_in")
        g_chunk_in = sem("g_chunk_in")
        g_chunk_free = sem("g_chunk_free")
        g_row_summed = sem("g_row_summed")
        g_transposed = sem("g_transposed")
        g_copied = sem("g_copied")
        g_partial = sem("g_partial")
        g_added = sem("g_added")
        g_dve = sem("g_dve")
        g_rows_ready = sem("g_rows_ready")
        g_pe = sem("g_pe")
        g_act = sem("g_act")
        g_out = sem("g_out")

        block = ctx.enter_context(nc.Block())

        x_rows = x.rearrange("(v p s) f -> p v (s f)", p=P, s=2)
        out_rows = out.rearrange("(v p s) f -> p v (s f)", p=P, s=2)
        adj_rows = adj.rearrange("(v p s) n -> p v s n", p=P, s=2)

        def block_columns(b):
            start = 2 * P * (b // 2) + b % 2
            return start, start + 2 * P - 1

        def in_pairs(rows):
            return rows.rearrange("p (v s) f -> p v (s f)", s=2)

        def apart(eng):
            eng.nop(nofuse=True)

        g_x = raw[0][:, 0:NB * D].rearrange("p (j f) -> p j f", f=D)
        g_x1 = raw[1][:, 0:NB * D].rearrange("p (j f) -> p j f", f=D)
        g_z = raw[2][:, 0:NB * D].rearrange("p (j f) -> p j f", f=D)
        g_chunk = raw[3][:, 0:GCH]
        g_chunkT = raw[3][:, GCH:2 * GCH]
        g_acc = agg[:, 0, :]
        g_rowsum = deg_inv[:, 1:2]

        @block.sync
        def _(sp):
            def load_half(t, c):
                s, half = c // 2, c % 2
                sp.dma_start(raw[c][:, :], adj_rows[:, ds(t, 1), s:s + 1, half * HALF:(half + 1) * HALF]
                             .rearrange("p a b n -> p (a b n)")).then_inc(raw_in[c], 16)

            load_half(0, 0)
            sp.dma_start(packw_f, packw_in).then_inc(const_in, 16)
            sp.dma_start(ident[:, :], ident_in).then_inc(const_in, 16)
            sp.dma_start(w0_sb, w0).then_inc(const_in, 16)
            sp.dma_start(w1_sb[:, :], w1).then_inc(const_in, 16)
            load_half(0, 1)
            sp.dma_start(in_pairs(resid[:, :, :]), x_rows).then_inc(x_in, 16)
            load_half(0, 2)
            load_half(0, 3)
            with sp.Fori(1, NPAIR) as t:
                for c in range(SLOTS):
                    sp.wait_ge(half_packed, SLOTS * t + (c + 1 - SLOTS))
                    sp.wait_ge(half_checked, SLOTS * t + (c + 1 - SLOTS))
                    sp.wait_ge(half_checked_act, SLOTS * t + (c + 1 - SLOTS))
                    load_half(t, c)

            def store_pair(v):
                sp.dma_start(out_rows[:, ds(v, 1), :], in_pairs(resid[:, ds(2 * v, 2), :])).then_inc(out_written, 16)

            with sp.Fori(0, NPAIR) as v:
                sp.wait_ge(normed, v + (NPAIR + 1))
                store_pair(v)
            sp.wait_ge(out_written, 16 * NPAIR)

            sp.wait_ge(flag_ready, 1)
            taken = sp.value_load(flag[0:1, 0:1], min_val=0, max_val=1)
            with sp.If(taken != 0):
                sp.dma_start(in_pairs(g_x), x_rows).then_inc(g_x_in, 16)
                sp.sem_inc(g_out, 16)
                for layer in range(2):
                    with sp.Fori(0, NPAIR) as v:
                        for s in range(2):
                            with sp.Fori(0, GN) as c:
                                n = v * (2 * GN) + c + (s + layer * NB) * GN
                                sp.wait_ge(g_chunk_free, n + 1)
                                sp.wait_ge(g_row_summed, n + 1)
                                sp.dma_start(g_chunk, adj_rows[:, ds(v, 1), s:s + 1, ds(c * GCH, GCH)]
                                             .rearrange("p a b n -> p (a b n)")).then_inc(g_chunk_in, 16)
                            if layer == 1:
                                sp.wait_ge(g_rows_ready, 2 * v + (s + 2))
                                sp.dma_start(out_rows[:, ds(v, 1), s * D:(s + 1) * D].rearrange("p a f -> p (a f)"),
                                             x1[:, 0, :]).then_inc(g_out, 16)
                sp.wait_ge(g_out, 16 * NB + 16)

        @block.tensor
        def _(pe):
            raw_hi = [r[:, :].bitcast(bf16) for r in raw]
            blocks = [spread[:, s, :, :, :].rearrange("p j s c -> p (j s c)").bitcast(fp8) for s in range(2)]

            def pack(t, s, halfway=None):
                if not isinstance(t, int) or t > 0:
                    pe.wait_ge(words_copied, 2 * t + (s - 1))
                for half in range(2):
                    c = 2 * s + half
                    pe.wait_ge(raw_in[c], 16 * t + 16)
                    for b in range(HB):
                        j = half * HB + b
                        n = PACKN if j * WPB + PACKN <= NB * WPB else WPB
                        lo, hi = block_columns(b)
                        last = nc.tensor.matmul(ps_words[s][:, j * WPB:j * WPB + n],
                                                raw_hi[c][:, 2 * lo + 1:2 * hi:4], packw[:, 0:n],
                                                start=True, stop=True)
                    last.then_inc(half_packed, 1)
                    if half == 0 and halfway is not None:
                        halfway()

            def product(t, s, known, early=None):
                pe.wait_ge(spread_done, 2 * t + (s + 1))
                if not isinstance(t, int) or t > 0:
                    pe.wait_ge(agg_read, 2 * t + (s - 1))
                apart(pe)
                for j in range(NB):
                    if j == NB // 8 and early is not None:
                        early()
                    w = XW + ZW if j < known else XW
                    last = nc.tensor.matmul(ps_agg[:, s, 0:w], blocks[s][:, j * P:(j + 1) * P], xz[:, j, 0:w],
                                            start=(j == 0), stop=(j == NB - 1))
                last.then_inc(product_done, 1)

            late_blocks = [late[:, s, :, :, :].rearrange("p j s c -> p (j s c)").bitcast(fp8) for s in range(2)]

            def catch_up(v, e, i):
                lo, hi = CATCH[e][i][1:]
                pe.wait_ge(late_spread, late_count(e, v, i) + 1)
                apart(pe)
                for s in range(2):
                    for j in range(lo, hi):
                        b = j - lo
                        last = nc.tensor.matmul(ps_late[:, s, 0:ZW], late_blocks[s][:, b * P:(b + 1) * P],
                                                xz[:, j, XW:XW + ZW], start=(b == 0), stop=(j == hi - 1))
                last.then_inc(late_product, 1)

            def last_sums(v, r, s, lo, hi, first=LAST):
                bank = (ps_agg, ps_late)[r]
                for j in range(lo, hi):
                    b = s * (NB // 2) + j - first
                    last = nc.tensor.matmul(bank[:, s, 0:ZW], blocks[r][:, b * P:(b + 1) * P],
                                            xz[:, j, XW:XW + ZW], start=(j == first), stop=(j == NB - 1))
                if hi == NB and s == 1:
                    last.then_inc(last_product, 1)

            def transpose_cat(w):
                pe.wait_ge(cat_written, w + 1)
                for s in range(2):
                    last = nc.tensor.transpose(ps_transposed[:, s * P:(s + 1) * P], cat[:, s, :], ident[:, :])
                last.then_inc(cat_transposed, 1)

            def linear0(w):
                pe.wait_ge(catT_copied, w + 1)
                if not isinstance(w, int) or w > 0:
                    pe.wait_ge(z_rest_made, w)
                for s in range(2):
                    last = nc.tensor.matmul(ps_linear[:, s * D:(s + 1) * D], catT[:, s * P:(s + 1) * P], w0T[:, :],
                                            start=True, stop=True)
                last.then_inc(lin0_done, 1)

            def transpose_x1(w):
                pe.wait_ge(normed, w + 1)
                apart(pe)
                for s in range(2):
                    last = nc.tensor.transpose(ps_transposed[0:D, s * P:(s + 1) * P], x1[:, s, :], ident[:, :])
                last.then_inc(x1_transposed, 1)

            def linear1(w):
                pe.wait_ge(x1T_copied, w + 1)
                for s in range(2):
                    last = nc.tensor.matmul(ps_linear[:, s * D:(s + 1) * D], x1T[:, s * P:(s + 1) * P], w1_sb[:, :],
                                            start=True, stop=True)
                last.then_inc(z_done, 1)

            def pair_body(v, e, more=True):
                late_pairs = len(CATCH[e])
                pack(v, 1, halfway=lambda: transpose_x1(v - 2))
                if late_pairs > 2:
                    catch_up(v, e, 0)
                product(v, 0, KNOWN_HALF[e], early=lambda: linear1(v - 2))
                if late_pairs > 1:
                    catch_up(v, e, late_pairs - 2)
                if more:
                    pack(v + 1, 0, halfway=lambda: transpose_cat(v - 1))
                else:
                    transpose_cat(v - 1)
                product(v, 1, KNOWN_HALF[e], early=lambda: linear0(v - 1))
                if not more:
                    transpose_x1(v - 1)
                if late_pairs > 0:
                    catch_up(v, e, late_pairs - 1)

            pe.wait_ge(consts_made, 3)
            pack(0, 0)
            pack(0, 1)
            pe.wait_ge(const_in, 16 * 4)
            nc.tensor.transpose(ps_transposed[:, 0:D], w0_sb, ident[0:D, 0:D]).then_inc(w0_transposed, 1)
            pe.wait_ge(w0T_copied, 1)
            pe.wait_ge(x_split, 2)
            product(0, 0, 0)
            pack(1, 0)
            product(0, 1, 0)
            pack(1, 1)
            product(1, 0, 0)
            transpose_cat(0)
            pack(2, 0)
            linear0(0)
            product(1, 1, 0)
            for e in range(HALVES):
                if KNOWN_HALF[e] > 0:
                    pe.wait_ge(z_stored, KNOWN_HALF[e] // 2)
                with pe.Fori(max(2, PPH * e), min(PPH * (e + 1), NPAIR - 1)) as v:
                    pair_body(v, e)
            v = NPAIR - 1
            pair_body(v, HALVES - 1, more=False)

            middle = LAST + LAG
            linear1(v - 1)
            transpose_cat(v)
            pe.wait_ge(last_spread, 1)
            pe.wait_ge(agg_read, NB)
            last_sums(0, 0, 0, LAST, middle)
            linear0(v)
            last_sums(0, 0, 0, middle, NB - LAG)
            last_sums(0, 0, 1, LAST, NB - LAG)
            pe.wait_ge(last_spread, 2)
            pe.wait_ge(late_read, LATE_BEFORE[HALVES])
            last_sums(1, 1, 0, LAST, middle)
            transpose_x1(v)
            last_sums(1, 1, 0, middle, NB - LAG)
            linear1(v)
            last_sums(1, 1, 1, LAST, NB - LAG)
            pe.wait_ge(z_stored, NPAIR)
            for first_pair in range(2):
                for s in range(2):
                    last_sums(first_pair, first_pair, s, NB - LAG, NB)
            pe.wait_ge(bad_counted, 1)
            nc.tensor.matmul(ps_linear[0:1, 0:1], bad_row[:, :], ones[:, :], start=True, stop=True)\
              .then_inc(bad_summed, 1)
            for lo, hi, first in ((1, (NPAIR - PPH) // 2, LAST), ((NPAIR - PPH) // 2, NPAIR // 2, LAST_HALF)):
                with pe.Fori(lo, hi) as q:
                    for r in range(2):
                        v = 2 * q + r
                        pe.wait_ge(last_spread, v + 1)
                        pe.wait_ge(last_read, v - 1)
                        apart(pe)
                        for s in range(2):
                            last_sums(v, r, s, first, NB, first)

            pe.wait_ge(flag_ready, 1)
            taken = pe.value_load(flag[0:1, 0:1], min_val=0, max_val=1)
            with pe.If(taken != 0):
                pe.wait_ge(out_written, 16 * NPAIR)
                pe.wait_ge(g_x_in, 16)
                pe.sem_inc(g_chunk_free, 1)
                for layer, source in enumerate((g_x, g_z)):
                    with pe.Fori(0, NB) as i:
                        with pe.Fori(0, GN) as c:
                            n = i * GN + c + layer * NB * GN
                            pe.wait_ge(g_chunk_in, 16 * n + 16)
                            pe.wait_ge(g_added, n + 1)
                            for q in range(GQ):
                                lo, hi = block_columns(q)
                                last = nc.tensor.transpose(ps_words[0][:, q * P:(q + 1) * P],
                                                           g_chunk[:, lo:hi:2], ident[:, :])
                            last.then_inc(g_chunk_free, 1)
                            pe.wait_ge(g_copied, n + 1)
                            for q in range(GQ):
                                last = nc.tensor.matmul(ps_agg[:, 0, 0:D], g_chunkT[:, q * P:(q + 1) * P],
                                                        source[:, ds(c * GQ + q, 1), :].rearrange("p a f -> p (a f)"),
                                                        start=(q == 0), stop=(q == GQ - 1))
                            last.then_inc(g_partial, 1)
                        if layer == 0:
                            pe.wait_ge(g_dve, 3 * i + 2)
                            nc.tensor.transpose(ps_transposed[:, 0:P], cat[:, 0, :], ident[:, :]).then_inc(g_pe, 1)
                            pe.wait_ge(g_act, 4 * i + 1)
                            nc.tensor.matmul(ps_linear[:, 0:D], catT[:, 0:P], w0T[:, :], start=True, stop=True)\
                              .then_inc(g_pe, 1)
                            pe.wait_ge(g_dve, 3 * i + 4)
                            apart(pe)
                            nc.tensor.transpose(ps_transposed[0:D, 0:P], x1[:, 0, :], ident[:, :]).then_inc(g_pe, 1)
                            pe.wait_ge(g_act, 4 * i + 3)
                            nc.tensor.matmul(ps_linear[:, 0:D], x1T[:, 0:P], w1_sb[:, :], start=True, stop=True)\
                              .then_inc(g_pe, 1)
                    if layer == 0:
                        pe.wait_ge(g_rows_ready, 1)

        @block.scalar
        def _(act):
            def copy_words(t, s, g):
                stripe_in_group = 2 * t + (s - SPG * g)
                act.wait_ge(half_packed, 4 * t + (2 * s + 2))
                if not isinstance(t, int) or 2 * t + s > 0:
                    act.wait_ge(spread_done, 2 * t + s)
                nc.scalar.activation(words_now[:, :], ps_words[s][:, :], ACT.Copy)
                nc.scalar.activation(words[g][:, ds(stripe_in_group, 1), :].rearrange("p a b -> p (a b)"),
                                     ps_words[s][:, KNOWN[g] * WPB:NB * WPB], ACT.Copy).then_inc(words_copied, 1)

            def copy_catT(w):
                act.wait_ge(cat_transposed, w + 1)
                nc.scalar.activation(catT[:, :], ps_transposed[:, 0:2 * P], ACT.Copy).then_inc(catT_copied, 1)

            def copy_x1T(w):
                act.wait_ge(x1_transposed, w + 1)
                nc.scalar.activation(x1T[:, :], ps_transposed[0:D, 0:2 * P], ACT.Copy).then_inc(x1T_copied, 1)

            def standard_deviation(n, r, eps):
                act.wait_ge(var_ready, n + 1)
                nc.scalar.activation(std[:, r, :], meanvar[:, r, :, 1], ACT.Sqrt, bias=eps[:, :]).then_inc(std_ready, 1)

            def store_z_hi(w):
                act.wait_ge(z_done, w + 1)
                nc.scalar.activation(xz[:, ds(2 * w, 2), XW:XW + D], ps_linear_v, ACT.Copy).then_inc(z_hi_stored, 1)

            upper = [r[:, 0:ACOLS].bitcast(u16)[:, 1::2] for r in raw]
            lower = [r[:, 0:ACOLS].bitcast(u16)[:, 0::2] for r in raw]

            def check(t, c):
                act.wait_ge(raw_in[c], 16 * t + 16)
                if not isinstance(t, int) or 4 * t + c > 0:
                    act.wait_ge(half_checked_act, 4 * t + c)
                apart(act)
                nc.scalar.activation(verdict[:, ACOLS:2 * ACOLS], upper[c], ACT.Relu,
                                     bias=minus_one_hi[:, :], scale=1.0 / DOWN,
                                     accum_out=above_one[:, ds(4 * t + c, 1)])
                nc.scalar.activation(verdict[:, 2 * ACOLS:3 * ACOLS], upper[c], ACT.Abs,
                                     bias=minus_middle[:, :], scale=1.0 / DOWN,
                                     accum_out=from_middle[:, ds(4 * t + c, 1)])
                nc.scalar.activation(verdict[:, 0:ACOLS], lower[c], ACT.Copy, scale=1.0 / DOWN,
                                     accum_out=low_bits[:, ds(4 * t + c, 1)]).then_inc(half_checked_act, 1)

            def pair_body(u, g):
                copy_catT(u - 2)
                check(u, 0)
                copy_words(u, 0, g)
                check(u, 1)
                standard_deviation(u - 2, 0, eps1)
                copy_x1T(u - 2)
                check(u, 2)
                copy_words(u, 1, g)
                store_z_hi(u - 2)
                check(u, 3)

            act.wait_ge(consts_made, 3)
            check(0, 0)
            check(0, 1)
            copy_words(0, 0, 0)
            act.wait_ge(x_in, 16)
            for q in range(2):
                nc.scalar.activation(xz[:, q * QX:(q + 1) * QX, 0:D], resid[:, q * QX:(q + 1) * QX, :], ACT.Copy)\
                  .then_inc(x_hi_stored, 1)
            for q in range(2):
                act.wait_ge(x_rest_made, q + 1)
                nc.scalar.activation(xz[:, q * QX:(q + 1) * QX, D:2 * D], x_rest[q], ACT.Copy)\
                  .then_inc(x_mid_stored, 1)
            check(0, 2)
            check(0, 3)
            copy_words(0, 1, 0)
            act.wait_ge(w0_transposed, 1)
            nc.scalar.activation(w0T[:, :], ps_transposed[:, 0:D], ACT.Copy).then_inc(w0T_copied, 1)
            check(1, 0)
            check(1, 1)
            copy_words(1, 0, 0)
            check(1, 2)
            check(1, 3)
            copy_words(1, 1, 0)
            for g in range(GROUPS):
                with act.Fori(max(2, g * PPG), (g + 1) * PPG) as u:
                    pair_body(u, g)
            w = NPAIR - 2
            copy_catT(w)
            standard_deviation(w, 0, eps1)
            copy_x1T(w)
            store_z_hi(w)
            copy_catT(w + 1)
            standard_deviation(w + 1, 0, eps1)
            copy_x1T(w + 1)
            store_z_hi(w + 1)
            with act.Fori(0, NPAIR // 2) as q:
                for r in range(2):
                    standard_deviation(2 * q + (r + NPAIR), r, eps4)

            act.wait_ge(flag_ready, 1)
            taken = act.value_load(flag[0:1, 0:1], min_val=0, max_val=1)
            with act.If(taken != 0):
                act.wait_ge(out_written, 16 * NPAIR)
                for layer in range(2):
                    with act.Fori(0, NB) as i:
                        with act.Fori(0, GN) as c:
                            n = i * GN + c + layer * NB * GN
                            act.wait_ge(g_chunk_free, n + 2)
                            nc.scalar.activation(g_chunkT, ps_words[0][:, :], ACT.Copy).then_inc(g_copied, 1)
                        if layer == 0:
                            act.wait_ge(g_pe, 4 * i + 1)
                            nc.scalar.activation(catT[:, 0:P], ps_transposed[:, 0:P], ACT.Copy).then_inc(g_act, 1)
                            act.wait_ge(g_dve, 3 * i + 3)
                            nc.scalar.activation(std[:, 0, 0:1], meanvar[:, 0, 0, 1:2], ACT.Sqrt, bias=eps1[:, :])\
                              .then_inc(g_act, 1)
                            act.wait_ge(g_pe, 4 * i + 3)
                            nc.scalar.activation(x1T[:, 0:P], ps_transposed[0:D, 0:P], ACT.Copy).then_inc(g_act, 1)
                            act.wait_ge(g_pe, 4 * i + 4)
                            nc.scalar.activation(g_z[:, ds(i, 1), :].rearrange("p a f -> p (a f)"), ps_linear[:, 0:D],
                                                 ACT.Copy).then_inc(g_act, 1)
                        else:
                            act.wait_ge(g_dve, i + (3 * NB + 2))
                            nc.scalar.activation(std[:, 0, 0:1], meanvar[:, 0, 0, 1:2], ACT.Sqrt, bias=eps1[:, :])\
                              .then_inc(g_act, 1)

        @block.vector
        def _(dve):
            now_lanes = words_now[:, :].bitcast(u32).rearrange("p (j c) -> p j c", c=UPB)

            def check(t, s, half):
                c = 2 * s + half
                dve.wait_ge(raw_in[c], 16 * t + 16)
                if not isinstance(t, int) or 4 * t + c > 0:
                    dve.wait_ge(half_checked, 4 * t + c)
                nc.vector.scalar_tensor_tensor(verdict[:, 3 * ACOLS:], raw[c][:, ACOLS:], 0.0, raw[c][:, ACOLS:],
                                               ALU.is_gt, ALU.not_equal,
                                               accum_out=bad[:, ds(4 * t + c, 1)]).then_inc(half_checked, 1)

            def spread_bits(out, lanes):
                for k in range(SHIFTS):
                    op = ALU.logical_shift_left if k <= TWO_FP8 else ALU.logical_shift_right
                    last = nc.vector.tensor_scalar(out(k), lanes, abs(TWO_FP8 - k), TWO_MASK, op, ALU.bitwise_and)
                return last

            def spread_now(t, s):
                dve.wait_ge(words_copied, 2 * t + (s + 1))
                if not isinstance(t, int) or t > 0:
                    dve.wait_ge(product_done, 2 * t + (s - 1))
                spread_bits(lambda k: spread[:, s, :, k, :], now_lanes).then_inc(spread_done, 1)

            def kept_lanes(g, pair, lo, hi):
                return words[g][:, ds(2 * pair, 2), (lo - KNOWN[g]) * WPB:(hi - KNOWN[g]) * WPB].bitcast(u32)\
                    .rearrange("p a (j c) -> p a j c", c=UPB)

            def read_late(n):
                dve.wait_ge(late_product, n + 1)
                if not isinstance(n, int) or n > 0:
                    dve.wait_ge(late_added, n)
                for s in range(2):
                    last = nc.vector.tensor_reduce(late_sum[:, s, :],
                                                   ps_late[:, s, 0:ZW].rearrange("p (k f) -> p f k", k=3),
                                                   axis=AX, op=ALU.add)
                last.then_inc(late_read, 1)

            def spread_late(u, e, i, first=False):
                if not first:
                    read_late(late_count(e, u, i - 1))
                k, lo, hi = CATCH[e][i]
                lanes = kept_lanes(k // 2, late_pair(e, u, i) - PPG * (k // 2), lo, hi)
                spread_bits(lambda b: late[:, :, 0:hi - lo, b, :], lanes).then_inc(late_spread, 1)

            def spread_last(v, r, g, lo=LAST):
                lanes = kept_lanes(g, v - PPG * g, lo, NB)
                out = spread[:, r, :, :, :].rearrange("p (a j) k c -> p a j k c", a=2)
                spread_bits(lambda k: out[:, :, 0:NB - lo, k, :], lanes).then_inc(last_spread, 1)

            def read_sums(w, s, with_z):
                dve.wait_ge(product_done, 2 * w + (s + 1))
                if s == 0 and (not isinstance(w, int) or w > 0):
                    dve.wait_ge(cat_written, w)
                nc.vector.tensor_reduce(agg[:, s, :], ps_agg[:, s, 0:3 * D].rearrange("p (k f) -> p f k", k=3),
                                        axis=AX, op=ALU.add)
                if with_z:
                    nc.vector.tensor_reduce(part[:, s, :], ps_agg[:, s, XW:XW + ZW].rearrange("p (k f) -> p f k", k=3),
                                            axis=AX, op=ALU.add)
                nc.vector.tensor_scalar(deg[:, s:s + 1], ps_agg[:, s, 3 * D:3 * D + 1], 2.0, None, ALU.max)\
                  .then_inc(agg_read, 1)

            def invert_degree(w):
                dve.wait_ge(agg_read, 2 * w + 2)
                nc.vector.reciprocal(deg_inv[:, :], deg[:, :]).then_inc(deg_inverted, 1)

            def moments(n, r):
                dve.wait_ge(h_written, n + 1)
                for s in range(2):
                    last = nc.vector.bn_stats(stats[:, s, :], hidden[r][:, s, :])
                last.then_inc(stats_written, 1)
                dve.wait_ge(stats_written, n + 1)
                apart(dve)
                for s in range(2):
                    last = nc.vector.bn_aggr(meanvar[:, r, s, :], stats[:, s, :])
                last.then_inc(var_ready, 1)

            def residual1(w):
                dve.wait_ge(lin0_done, w + 1)
                nc.vector.scalar_tensor_tensor(hidden[0][:, :, :], ps_linear_v, 0.0, resid[:, ds(2 * w, 2), :],
                                               ALU.max, ALU.add)\
                  .then_inc(h_written, 1)
                moments(w, 0)

            def invert_std(n, r=0):
                dve.wait_ge(std_ready, n + 1)
                nc.vector.reciprocal(rstd[:, r, :], std[:, r, :]).then_inc(rstd_ready, 1)

            def z_minus_hi(w):
                dve.wait_ge(z_hi_stored, w + 1)
                nc.vector.tensor_tensor(z_rest[:, :, :], ps_linear_v, xz[:, ds(2 * w, 2), XW:XW + D], ALU.subtract)\
                  .then_inc(z_rest_made, 1)

            def pair_body(u, e, first=False):
                with_z = e > 1 or (e == 1 and not first)
                late_pairs = len(CATCH[e])
                for half in range(2):
                    check(u, 0, half)
                residual1(u - 2)
                spread_now(u, 0)
                invert_std(u - 2)
                read_sums(u - 1, 0, with_z)
                if late_pairs > 2:
                    spread_late(u, e, 0)
                check(u, 1, 0)
                if late_pairs > 1:
                    spread_late(u, e, late_pairs - 2, first and late_pairs == 2)
                check(u, 1, 1)
                z_minus_hi(u - 2)
                spread_now(u, 1)
                read_sums(u - 1, 1, with_z)
                invert_degree(u - 1)
                if late_pairs > 0:
                    spread_late(u, e, late_pairs - 1)

            nc.vector.memset(minus_one_hi[:, :], -float(ONE_HI // DOWN))
            nc.vector.memset(minus_middle[:, :], -float(ONE_HI // DOWN // 2))
            nc.vector.memset(ones[:, :], 1.0)
            nc.vector.memset(eps1[:, :], EPS).then_inc(consts_made, 1)
            nc.vector.memset(eps4[:, :], 4 * EPS).then_inc(consts_made, 1)
            nc.vector.memset(xz[:, :, 3 * D:3 * D + 1], 1.0)
            dve.wait_ge(const_in, 16 * 4)
            nc.vector.tensor_copy(packw[:, :], packw_f).then_inc(consts_made, 1)
            for half in range(2):
                check(0, 0, half)
            spread_now(0, 0)
            for q in range(2):
                dve.wait_ge(x_hi_stored, q + 1)
                nc.vector.tensor_tensor(x_rest[q], resid[:, q * QX:(q + 1) * QX, :], xz[:, q * QX:(q + 1) * QX, 0:D],
                                        ALU.subtract).then_inc(x_rest_made, 1)
            for q in range(2):
                dve.wait_ge(x_mid_stored, q + 1)
                nc.vector.tensor_tensor(xz[:, q * QX:(q + 1) * QX, 2 * D:3 * D], x_rest[q],
                                        xz[:, q * QX:(q + 1) * QX, D:2 * D], ALU.subtract).then_inc(x_split, 1)
            for half in range(2):
                check(0, 1, half)
            spread_now(0, 1)
            for half in range(2):
                check(1, 0, half)
            spread_now(1, 0)
            read_sums(0, 0, False)
            for half in range(2):
                check(1, 1, half)
            spread_now(1, 1)
            read_sums(0, 1, False)
            invert_degree(0)
            with dve.Fori(2, PPH) as u:
                pair_body(u, 0)
            for e in (1, 2):
                pair_body(PPH * e, e, first=True)
                with dve.Fori(PPH * e + 1, PPH * (e + 1)) as u:
                    pair_body(u, e)
            for e in range(3, HALVES):
                with dve.Fori(PPH * e, PPH * (e + 1)) as u:
                    pair_body(u, e)
            w = NPAIR - 2
            dve.wait_ge(half_checked, 4 * NPAIR)
            dve.wait_ge(half_checked_act, 4 * NPAIR)
            for n, (sums, right_sum) in enumerate(((from_middle, float(ACOLS * (ONE_HI // DOWN // 2))),
                                                   (above_one, 0.0), (low_bits, 0.0))):
                nc.vector.scalar_tensor_tensor(bad[:, :], sums[:, :], right_sum, bad[:, :], ALU.not_equal, ALU.add)\
                  .then_inc(bad_listed, 1)
                dve.wait_ge(bad_listed, n + 1)
            nc.vector.tensor_reduce(bad_row[:, :], bad[:, :], axis=AX, op=ALU.add).then_inc(bad_counted, 1)
            residual1(w)
            dve.wait_ge(product_done, NB - 1)
            spread_last(0, 0, 0)
            invert_std(w)
            read_sums(w + 1, 0, True)
            read_sums(w + 1, 1, True)
            invert_degree(w + 1)
            spread_last(1, 1, 0)
            read_late(LATE_BEFORE[HALVES] - 1)
            z_minus_hi(w)
            residual1(w + 1)
            invert_std(w + 1)
            z_minus_hi(w + 1)

            def read_last(v, r):
                bank = (ps_agg, ps_late)[r]
                dve.wait_ge(last_product, v + 1)
                for s in range(2):
                    last = nc.vector.tensor_reduce(agg[:, s, :], bank[:, s, 0:ZW].rearrange("p (k f) -> p f k", k=3),
                                                   axis=AX, op=ALU.add)
                last.then_inc(last_read, 1)

            def residual2(v, r, invert_before=True):
                dve.wait_ge(last_read, v + 1)
                dve.wait_ge(normed, v + (NPAIR - 1))
                nc.vector.tensor_tensor(hidden[r][:, :, :], agg[:, :, :], resid[:, ds(2 * v, 2), :], ALU.add)\
                  .then_inc(h_written, 1)
                if invert_before:
                    invert_std(v - 1 + NPAIR, 1 - r)
                moments(v + NPAIR, r)

            def pair_body2(v, r, g, lo=LAST, first=False):
                if first:
                    dve.wait_ge(last_product, v - 1)
                    spread_last(v, r, g, lo)
                read_last(v - 2, r)
                if not first:
                    spread_last(v, r, g, lo)
                residual2(v - 2, r, not first)

            dve.wait_ge(resid_written, NPAIR)
            dve.wait_ge(late_added, LATE_BEFORE[HALVES])
            pair_body2(2, 0, 0, first=True)
            pair_body2(3, 1, 0)
            for e in range(1, HALVES):
                with dve.Fori(PPH * e // 2, PPH * (e + 1) // 2) as q:
                    for r in range(2):
                        pair_body2(2 * q + r, r, e // 2, LAST_HALF if e == HALVES - 1 else LAST)
            dve.wait_ge(bad_summed, 1)
            nc.vector.tensor_scalar(flag[:, :], ps_linear[0:1, 0:1], 0.0, None, ALU.is_gt).then_inc(flag_ready, 1)
            read_last(NPAIR - 2, 0)
            residual2(NPAIR - 2, 0)
            read_last(NPAIR - 1, 1)
            residual2(NPAIR - 1, 1)
            invert_std(2 * NPAIR - 1, 1)

            dve.wait_ge(flag_ready, 1)
            taken = dve.value_load(flag[0:1, 0:1], min_val=0, max_val=1)
            with dve.If(taken != 0):
                dve.wait_ge(out_written, 16 * NPAIR)
                dve.wait_ge(g_x_in, 16)
                dve.sem_inc(g_row_summed, 1)
                dve.sem_inc(g_added, 1)
                nc.vector.memset(deg_inv[:, :], 0.0).then_inc(g_dve, 1)

                def g_normalise(rows, m):
                    nc.vector.bn_stats(stats[:, 0, :], hidden[0][:, 0, :]).then_inc(stats_written, 1)
                    dve.drain()
                    nc.vector.bn_aggr(meanvar[:, 0, 0, :], stats[:, 0, :]).then_inc(g_dve, 1)
                    dve.wait_ge(g_act, m)
                    nc.vector.reciprocal(rstd[:, 0, 0:1], std[:, 0, 0:1])
                    dve.drain()
                    return nc.vector.tensor_scalar(rows, hidden[0][:, 0, :], meanvar[:, 0, 0, 0:1], rstd[:, 0, 0:1],
                                                   ALU.subtract, ALU.mult)

                for layer in range(2):
                    with dve.Fori(0, NB) as i:
                        nc.vector.memset(g_acc, 0.0)
                        nc.vector.memset(deg[:, 0:1], 0.0)
                        dve.drain()
                        with dve.Fori(0, GN) as c:
                            n = i * GN + c + layer * NB * GN
                            dve.wait_ge(g_chunk_in, 16 * n + 16)
                            nc.vector.tensor_reduce(g_rowsum, g_chunk, axis=AX, op=ALU.add).then_inc(g_row_summed, 1)
                            dve.drain()
                            nc.vector.tensor_tensor(deg[:, 0:1], deg[:, 0:1], g_rowsum, ALU.add)
                            dve.wait_ge(g_partial, n + 1)
                            nc.vector.tensor_tensor(g_acc, g_acc, ps_agg[:, 0, 0:D], ALU.add).then_inc(g_added, 1)
                            dve.drain()
                        if layer == 0:
                            nc.vector.tensor_scalar(deg[:, 1:2], deg[:, 0:1], 1.0, None, ALU.max)
                            dve.drain()
                            nc.vector.reciprocal(deg_inv[:, 0:1], deg[:, 1:2])
                            nc.vector.tensor_copy(cat[:, 0, 0:D], g_x[:, ds(i, 1), :].rearrange("p a f -> p (a f)"))
                            dve.drain()
                            nc.vector.tensor_scalar(cat[:, 0, D:2 * D], g_acc, deg_inv[:, 0:1], None, ALU.mult)\
                              .then_inc(g_dve, 1)
                            dve.wait_ge(g_pe, 4 * i + 2)
                            nc.vector.scalar_tensor_tensor(hidden[0][:, 0, :], ps_linear[:, 0:D], 0.0,
                                                           g_x[:, ds(i, 1), :].rearrange("p a f -> p (a f)"),
                                                           ALU.max, ALU.add)
                            dve.drain()
                            g_normalise(x1[:, 0, :], 4 * i + 2).then_inc(g_dve, 1)
                            dve.drain()
                            nc.vector.tensor_copy(g_x1[:, ds(i, 1), :].rearrange("p a f -> p (a f)"), x1[:, 0, :])
                            dve.wait_ge(g_act, 4 * i + 4)
                        else:
                            nc.vector.tensor_tensor(hidden[0][:, 0, :], g_acc,
                                                    g_x1[:, ds(i, 1), :].rearrange("p a f -> p (a f)"), ALU.add)
                            dve.drain()
                            g_normalise(x1_twice[:, 0, :], i + (4 * NB + 1))
                            dve.drain()
                            dve.wait_ge(g_out, 16 * i + 16)
                            nc.vector.tensor_copy(x1[:, 0, :], x1_twice[:, 0, :]).then_inc(g_rows_ready, 1)
                    if layer == 0:
                        nc.vector.memset(x1[:, 1, :], 0.0).then_inc(g_rows_ready, 1)

        @block.gpsimd
        def _(pool):
            def write_cat(w, with_z):
                pool.wait_ge(deg_inverted, w + 1)
                if not isinstance(w, int) or w > 0:
                    pool.wait_ge(cat_transposed, w)
                if with_z:
                    pool.wait_ge(resid_written, w)
                apart(pool)
                if with_z:
                    nc.gpsimd.tensor_copy(part_kept[:, :, :], part[:, :, :])
                nc.gpsimd.tensor_copy(cat[:, :, 0:D], resid[:, ds(2 * w, 2), :])
                nc.gpsimd.tensor_tensor(cat[:, :, D:2 * D], agg[:, :, :],
                                        deg_inv[:, :].unsqueeze(2).to_broadcast([P, 2, D]), ALU.mult)\
                  .then_inc(cat_written, 1)

            def normalise(n):
                pool.wait_ge(rstd_ready, n + 1)
                apart(pool)
                nc.gpsimd.tensor_tensor(x1[:, :, :], hidden[0][:, :, :], meanvar[:, 0, :, 0:1].to_broadcast([P, 2, D]),
                                        ALU.subtract).then_inc(centred, 1)
                pool.wait_ge(centred, n + 1)
                apart(pool)
                nc.gpsimd.tensor_tensor(x1[:, :, :], x1[:, :, :], rstd[:, 0, :].unsqueeze(2).to_broadcast([P, 2, D]),
                                        ALU.mult).then_inc(normed, 1)

            def keep_x1(w, with_z):
                normalise(w)
                pool.wait_ge(normed, w + 1)
                apart(pool)
                if with_z:
                    nc.gpsimd.tensor_tensor(x1_twice[:, :, :], x1[:, :, :], x1[:, :, :], ALU.add)\
                      .then_inc(x1_doubled, 1)
                    pool.wait_ge(x1_doubled, w - (PPH - 1))
                    apart(pool)
                    nc.gpsimd.tensor_tensor(resid[:, ds(2 * w, 2), :], x1_twice[:, :, :], part_kept[:, :, :], ALU.add)\
                      .then_inc(resid_written, 1)
                else:
                    nc.gpsimd.tensor_tensor(resid[:, ds(2 * w, 2), :], x1[:, :, :], x1[:, :, :], ALU.add)\
                      .then_inc(resid_written, 1)

            def store_z(w):
                pool.wait_ge(z_rest_made, w + 1)
                apart(pool)
                nc.gpsimd.tensor_copy(xz[:, ds(2 * w, 2), XW + D:XW + 2 * D], z_rest[:, :, :])\
                  .then_inc(z_mid_stored, 1)
                pool.wait_ge(z_mid_stored, w + 1)
                apart(pool)
                nc.gpsimd.tensor_tensor(xz[:, ds(2 * w, 2), XW + 2 * D:XW + 3 * D], z_rest[:, :, :],
                                        xz[:, ds(2 * w, 2), XW + D:XW + 2 * D], ALU.subtract).then_inc(z_stored, 1)

            def add_late(n, pair):
                pool.wait_ge(late_read, n + 1)
                apart(pool)
                rows = resid[:, ds(2 * pair, 2), :]
                nc.gpsimd.tensor_tensor(rows, rows, late_sum[:, :, :], ALU.add).then_inc(late_added, 1)

            def add_late_of(e, u, i):
                add_late(late_count(e, u, i), late_pair(e, u, i))

            def pair_body(u, e, first=False, z_before=True, z_before2=True):
                late_pairs = len(CATCH[e])
                e_before = e - 1 if first else e
                keep_x1(u - 2, z_before2)
                if late_pairs > 1 and CATCH[e_before]:
                    add_late_of(e_before, u - 1, len(CATCH[e_before]) - 1)
                if late_pairs > 2:
                    add_late_of(e, u, 0)
                store_z(u - 2)
                write_cat(u - 1, z_before)
                if late_pairs > 1:
                    add_late_of(e, u, late_pairs - 2)

            write_cat(0, False)
            with pool.Fori(2, PPH + 1) as u:
                pair_body(u, 0, z_before=False, z_before2=False)
            pair_body(PPH + 1, 1, z_before2=False)
            with pool.Fori(PPH + 2, 2 * PPH) as u:
                pair_body(u, 1)
            for e in range(2, HALVES):
                pair_body(PPH * e, e, first=True)
                with pool.Fori(PPH * e + 1, PPH * (e + 1)) as u:
                    pair_body(u, e)
            keep_x1(NPAIR - 2, True)
            write_cat(NPAIR - 1, True)
            add_late_of(HALVES - 1, NPAIR - 1, len(CATCH[HALVES - 1]) - 1)
            store_z(NPAIR - 2)
            keep_x1(NPAIR - 1, True)
            store_z(NPAIR - 1)

            def normalise_last(v, r):
                pool.wait_ge(rstd_ready, v + (NPAIR + 1))
                pool.wait_ge(normed, v + NPAIR)
                apart(pool)
                nc.gpsimd.tensor_tensor(x1[:, :, :], hidden[r][:, :, :], meanvar[:, r, :, 0:1].to_broadcast([P, 2, D]),
                                        ALU.subtract).then_inc(centred, 1)
                pool.wait_ge(centred, v + (NPAIR + 1))
                apart(pool)
                nc.gpsimd.tensor_tensor(resid[:, ds(2 * v, 2), :], x1[:, :, :],
                                        rstd[:, r, :].unsqueeze(2).to_broadcast([P, 2, D]), ALU.mult)\
                  .then_inc(normed, 1)

            pool.wait_ge(x1_transposed, NPAIR)
            with pool.Fori(0, NPAIR // 2) as q:
                for r in range(2):
                    normalise_last(2 * q + r, r)


_INS = ['x', 'adj', 'L0_gnn_W', 'L1_gnn_weight']


def kernel(**inputs):
    import numpy as _np
    import concourse.bacc as _bacc
    from concourse import mybir as _mybir
    from concourse.bass_utils import run_bass_kernel_spmd as _run

    nc = _bacc.Bacc("TRN2", target_bir_lowering=False, num_devices=1)
    arrays, args = {}, []
    named = [(name, _np.ascontiguousarray(inputs[name])) for name in _INS]
    named += [("pack_weights", pack_weights()), ("identity", _np.eye(P, dtype=_np.float32))]
    for name, a in named:
        arrays[f"in_{name}_dram"] = a
        args.append(nc.dram_tensor(f"in_{name}_dram", a.shape, _mybir.dt.from_np(a.dtype), kind="ExternalInput").ap())
    args.append(nc.dram_tensor("out_0_dram", (N, D), _mybir.dt.float32, kind="ExternalOutput").ap())
    gnn_kernel(nc, *args)
    r = _run(nc, [arrays], core_ids=[0])
    return r.results[0]["out_0_dram"]
```
